# Optimizing a Trainium2 kernel written in Bass

```python
import numpy as np
import jax
import jax.numpy as jnp

def _softmax(x, axis=-1):
    return jax.nn.softmax(x, axis=axis)
def _gelu(x):
    return jax.nn.gelu(x, approximate=True)
def _silu(x):
    return jax.nn.silu(x)
def _sigmoid(x):
    return jax.nn.sigmoid(x)
def _layernorm(x, axis=-1, eps=1e-5):
    m = jnp.mean(x, axis=axis, keepdims=True)
    v = jnp.var(x, axis=axis, keepdims=True)
    return (x - m) / jnp.sqrt(v + eps)
def _scatter_add(tgt, idx, src, axis=0):
    return tgt.at[idx].add(src)
def _segment_sum(src, seg, n):
    return jax.ops.segment_sum(src, seg, n)

kernel_name = 'mk_conv_preact_d1_conv_nhwc256_173335'

def setup_inputs(seed: int = 0):
    np.random.seed(seed)
    _w = jnp.asarray
    def _rec_inputs():
        import jax
        import jax.numpy as jnp
        _gk = jax.random.key(seed)
        x = -0.0003929 + 0.9999 * jax.random.normal(jax.random.fold_in(_gk, 1), (4, 64, 256, 256), jnp.float32)
        return x
    x = _rec_inputs()
    def _L0_conv_setup():
        import jax, jax.numpy as jnp
        import numpy as np
        EPS = 1e-05
        SCALE = 4

        def _inorm(x, w, b):
            mu = x.mean(axis=(-2, -1), keepdims=True)
            var = x.var(axis=(-2, -1), keepdims=True)
            return (x - mu) / jnp.sqrt(var + EPS) * w[None, :, None, None] + b[None, :, None, None]

        def _cplx(w):
            return jax.lax.complex(w[..., 0], w[..., 1])

        def _spec_conv(x, w1, w2, out_hw, bias=None):
            B, Ci, H, W = x.shape
            xf = jnp.fft.rfft2(x, norm='forward')
            m1, m2 = (w1.shape[2], w1.shape[3])
            Ho, Wo = out_hw
            Co = w1.shape[1]
            top = jnp.einsum('bixy,ioxy->boxy', xf[:, :, :m1, :m2], w1)
            bot = jnp.einsum('bixy,ioxy->boxy', xf[:, :, H - m1:, :m2], w2)
            out_ft = jnp.zeros((B, Co, Ho, Wo // 2 + 1), dtype=xf.dtype)
            out_ft = out_ft.at[:, :, :m1, :m2].set(top)
            out_ft = out_ft.at[:, :, Ho - m1:, :m2].set(bot)
            y = jnp.fft.irfft2(out_ft, s=(Ho, Wo), norm='forward')
            if bias is not None:
                y = y + bias[None, :, None, None]
            return y

        def tno_forward(x, kw1, kw2, qw1, qw2, vw1, vw2, mix_w1, mix_w2, mix_bias, mix_skip_w, mix_skip_b, mix_norm_w, mix_norm_b, norm1_w, norm1_b, an_w, an_b, norm2_w, norm2_b, mon_w, mon_b):
            B, C, H, W = x.shape
            xa = x.reshape(B * C, 1, H, W)
            xa_n = _inorm(xa, norm1_w, norm1_b)
            hk, wk = (H // SCALE, W // SCALE)
            k = _spec_conv(xa_n, _cplx(kw1), _cplx(kw2), (hk, wk))
            q = _spec_conv(xa_n, _cplx(qw1), _cplx(qw2), (hk, wk))
            v = _spec_conv(xa_n, _cplx(vw1), _cplx(vw2), (H, W))
            q = q.reshape(B, C, hk * wk)[:, None]
            k = k.reshape(B, C, hk * wk)[:, None]
            v = v.reshape(B, C, H * W)[:, None]
            dprod = jnp.einsum('batd,basd->bats', q, k) * jnp.sqrt(jnp.float32(hk * wk))
            dprod = jax.nn.softmax(dprod, axis=-1)
            att = jnp.einsum('bats,basd->batd', dprod, v)
            att = att.reshape(B * C, 1, H, W)
            att = _inorm(att, an_w, an_b) + xa
            att_n = _inorm(att, norm2_w, norm2_b)
            mix = _spec_conv(att_n, _cplx(mix_w1), _cplx(mix_w2), (H, W), bias=mix_bias)
            skip = jnp.einsum('bihw,oi->bohw', att_n, mix_skip_w) + mix_skip_b[None, :, None, None]
            mixed = _inorm(mix + skip, mix_norm_w, mix_norm_b)
            out = _inorm(mixed, mon_w, mon_b) + att
            return out.reshape(B, C, H, W)
        key = jax.random.key(seed)
        ks = jax.random.split(key, 10)
        B, C, H, W = (4, 64, 256, 256)
        mk, mm = (8, 32)
        s = 0.02
        f32 = jnp.float32
        one = jnp.ones((1,), f32)
        zero = jnp.zeros((1,), f32)
        return {'x': jax.random.normal(ks[0], (B, C, H, W), f32), 'kw1': s * jax.random.normal(ks[1], (1, 1, mk, mk, 2), f32), 'kw2': s * jax.random.normal(ks[2], (1, 1, mk, mk, 2), f32), 'qw1': s * jax.random.normal(ks[3], (1, 1, mk, mk, 2), f32), 'qw2': s * jax.random.normal(ks[4], (1, 1, mk, mk, 2), f32), 'vw1': s * jax.random.normal(ks[5], (1, 1, mk, mk, 2), f32), 'vw2': s * jax.random.normal(ks[6], (1, 1, mk, mk, 2), f32), 'mix_w1': s * jax.random.normal(ks[7], (1, 1, mm, mm, 2), f32), 'mix_w2': s * jax.random.normal(ks[8], (1, 1, mm, mm, 2), f32), 'mix_bias': zero, 'mix_skip_w': jax.random.normal(ks[9], (1, 1), f32), 'mix_skip_b': zero, 'mix_norm_w': one, 'mix_norm_b': zero, 'norm1_w': one, 'norm1_b': zero, 'an_w': one, 'an_b': zero, 'norm2_w': one, 'norm2_b': zero, 'mon_w': one, 'mon_b': zero}
    _L0_conv_all = _L0_conv_setup()
    _L0_conv_in = {k: v for k, v in _L0_conv_all.items() if k in ('kw1', 'kw2', 'qw1', 'qw2', 'vw1', 'vw2', 'mix_w1', 'mix_w2', 'mix_bias', 'mix_skip_w', 'mix_skip_b', 'mix_norm_w', 'mix_norm_b', 'norm1_w', 'norm1_b', 'an_w', 'an_b', 'norm2_w', 'norm2_b', 'mon_w', 'mon_b', )}
    del _L0_conv_all

    return {
        "x": x,
        "L0_conv_kw1": _L0_conv_in["kw1"],
        "L0_conv_kw2": _L0_conv_in["kw2"],
        "L0_conv_qw1": _L0_conv_in["qw1"],
        "L0_conv_qw2": _L0_conv_in["qw2"],
        "L0_conv_vw1": _L0_conv_in["vw1"],
        "L0_conv_vw2": _L0_conv_in["vw2"],
        "L0_conv_mix_w1": _L0_conv_in["mix_w1"],
        "L0_conv_mix_w2": _L0_conv_in["mix_w2"],
        "L0_conv_mix_bias": _L0_conv_in["mix_bias"],
        "L0_conv_mix_skip_w": _L0_conv_in["mix_skip_w"],
        "L0_conv_mix_skip_b": _L0_conv_in["mix_skip_b"],
        "L0_conv_mix_norm_w": _L0_conv_in["mix_norm_w"],
        "L0_conv_mix_norm_b": _L0_conv_in["mix_norm_b"],
        "L0_conv_norm1_w": _L0_conv_in["norm1_w"],
        "L0_conv_norm1_b": _L0_conv_in["norm1_b"],
        "L0_conv_an_w": _L0_conv_in["an_w"],
        "L0_conv_an_b": _L0_conv_in["an_b"],
        "L0_conv_norm2_w": _L0_conv_in["norm2_w"],
        "L0_conv_norm2_b": _L0_conv_in["norm2_b"],
        "L0_conv_mon_w": _L0_conv_in["mon_w"],
        "L0_conv_mon_b": _L0_conv_in["mon_b"],
    }

def reference(x, L0_conv_kw1, L0_conv_kw2, L0_conv_qw1, L0_conv_qw2, L0_conv_vw1, L0_conv_vw2, L0_conv_mix_w1, L0_conv_mix_w2, L0_conv_mix_bias, L0_conv_mix_skip_w, L0_conv_mix_skip_b, L0_conv_mix_norm_w, L0_conv_mix_norm_b, L0_conv_norm1_w, L0_conv_norm1_b, L0_conv_an_w, L0_conv_an_b, L0_conv_norm2_w, L0_conv_norm2_b, L0_conv_mon_w, L0_conv_mon_b):
    import jax
    import jax.numpy as jnp
    def _L0_conv_ref(x, kw1, kw2, qw1, qw2, vw1, vw2, mix_w1, mix_w2, mix_bias, mix_skip_w, mix_skip_b, mix_norm_w, mix_norm_b, norm1_w, norm1_b, an_w, an_b, norm2_w, norm2_b, mon_w, mon_b):
        import jax, jax.numpy as jnp
        import numpy as np
        EPS = 1e-05
        SCALE = 4

        def _inorm(x, w, b):
            mu = x.mean(axis=(-2, -1), keepdims=True)
            var = x.var(axis=(-2, -1), keepdims=True)
            return (x - mu) / jnp.sqrt(var + EPS) * w[None, :, None, None] + b[None, :, None, None]

        def _cplx(w):
            return jax.lax.complex(w[..., 0], w[..., 1])

        def _spec_conv(x, w1, w2, out_hw, bias=None):
            B, Ci, H, W = x.shape
            xf = jnp.fft.rfft2(x, norm='forward')
            m1, m2 = (w1.shape[2], w1.shape[3])
            Ho, Wo = out_hw
            Co = w1.shape[1]
            top = jnp.einsum('bixy,ioxy->boxy', xf[:, :, :m1, :m2], w1)
            bot = jnp.einsum('bixy,ioxy->boxy', xf[:, :, H - m1:, :m2], w2)
            out_ft = jnp.zeros((B, Co, Ho, Wo // 2 + 1), dtype=xf.dtype)
            out_ft = out_ft.at[:, :, :m1, :m2].set(top)
            out_ft = out_ft.at[:, :, Ho - m1:, :m2].set(bot)
            y = jnp.fft.irfft2(out_ft, s=(Ho, Wo), norm='forward')
            if bias is not None:
                y = y + bias[None, :, None, None]
            return y

        def tno_forward(x, kw1, kw2, qw1, qw2, vw1, vw2, mix_w1, mix_w2, mix_bias, mix_skip_w, mix_skip_b, mix_norm_w, mix_norm_b, norm1_w, norm1_b, an_w, an_b, norm2_w, norm2_b, mon_w, mon_b):
            B, C, H, W = x.shape
            xa = x.reshape(B * C, 1, H, W)
            xa_n = _inorm(xa, norm1_w, norm1_b)
            hk, wk = (H // SCALE, W // SCALE)
            k = _spec_conv(xa_n, _cplx(kw1), _cplx(kw2), (hk, wk))
            q = _spec_conv(xa_n, _cplx(qw1), _cplx(qw2), (hk, wk))
            v = _spec_conv(xa_n, _cplx(vw1), _cplx(vw2), (H, W))
            q = q.reshape(B, C, hk * wk)[:, None]
            k = k.reshape(B, C, hk * wk)[:, None]
            v = v.reshape(B, C, H * W)[:, None]
            dprod = jnp.einsum('batd,basd->bats', q, k) * jnp.sqrt(jnp.float32(hk * wk))
            dprod = jax.nn.softmax(dprod, axis=-1)
            att = jnp.einsum('bats,basd->batd', dprod, v)
            att = att.reshape(B * C, 1, H, W)
            att = _inorm(att, an_w, an_b) + xa
            att_n = _inorm(att, norm2_w, norm2_b)
            mix = _spec_conv(att_n, _cplx(mix_w1), _cplx(mix_w2), (H, W), bias=mix_bias)
            skip = jnp.einsum('bihw,oi->bohw', att_n, mix_skip_w) + mix_skip_b[None, :, None, None]
            mixed = _inorm(mix + skip, mix_norm_w, mix_norm_b)
            out = _inorm(mixed, mon_w, mon_b) + att
            return out.reshape(B, C, H, W)
        return tno_forward(x, kw1, kw2, qw1, qw2, vw1, vw2, mix_w1, mix_w2, mix_bias, mix_skip_w, mix_skip_b, mix_norm_w, mix_norm_b, norm1_w, norm1_b, an_w, an_b, norm2_w, norm2_b, mon_w, mon_b)

    def _gn(v, G=32, eps=1e-5):
        B_, H_, W_, C_ = v.shape
        g = v.reshape(B_, H_, W_, G, C_ // G)
        m = jnp.mean(g, axis=(1, 2, 4), keepdims=True)
        s = jnp.var(g, axis=(1, 2, 4), keepdims=True)
        return ((g - m) / jnp.sqrt(s + eps)).reshape(v.shape)

    def _ln_c(v, eps=1e-6):
        m = jnp.mean(v, axis=-1, keepdims=True)
        s = jnp.var(v, axis=-1, keepdims=True)
        return (v - m) / jnp.sqrt(s + eps)

    def _ln_t(v, eps=1e-5):
        m = jnp.mean(v, axis=-1, keepdims=True)
        s = jnp.var(v, axis=-1, keepdims=True)
        return (v - m) / jnp.sqrt(s + eps)

    def _to_tokens(v):
        B_, H_, W_, C_ = v.shape
        return v.reshape(B_, H_ * W_, C_)
    def _from_tokens(t, like):
        return t.reshape(like.shape)

    x = x + _L0_conv_ref(_gn(x), L0_conv_kw1, L0_conv_kw2, L0_conv_qw1, L0_conv_qw2, L0_conv_vw1, L0_conv_vw2, L0_conv_mix_w1, L0_conv_mix_w2, L0_conv_mix_bias, L0_conv_mix_skip_w, L0_conv_mix_skip_b, L0_conv_mix_norm_w, L0_conv_mix_norm_b, L0_conv_norm1_w, L0_conv_norm1_b, L0_conv_an_w, L0_conv_an_b, L0_conv_norm2_w, L0_conv_norm2_b, L0_conv_mon_w, L0_conv_mon_b)
    return x


_drawn_inputs = setup_inputs


def setup_inputs(seed=0):
    import zlib

    import numpy as np

    out = dict(_drawn_inputs(seed))
    spreads = {}
    factors = {'L0_conv_kw1': 8.0, 'L0_conv_kw2': 8.0, 'L0_conv_qw1': 8.0, 'L0_conv_qw2': 8.0}
    for name, (base, spread) in spreads.items():
        noise = np.random.default_rng([zlib.crc32(name.encode()), seed]).standard_normal(out[name].shape)
        drawn = base * np.exp(spread * noise) if base else spread * noise
        out[name] = jnp.asarray(drawn.astype(out[name].dtype))
    for name, factor in factors.items():
        out[name] = (out[name] * factor).astype(out[name].dtype)
    return out
```

```python
import numpy as np
from contextlib import ExitStack

import concourse.bass as bass
from concourse import mybir

B, IMGS, H, W = 4, 64, 256, 256
GROUPS, GW = 32, 8
HC = WC = 2
NU, NV = 64, 32
LU, LV = 17, 8
LOW = LU * LV
YC = 33 + 32
HALF = 4
G = 8
NG = IMGS // G
PAIRS = IMGS // 2
PG = G // 2
CHUNK = 4
NQ = IMGS // CHUNK
LAG = 2
EPS = 1e-5
LOGIT_SCALE = float(64 * 64) * 64.0
SCALARS = 9
SC_N1W, SC_N1B, SC_AW, SC_N2W, SC_K, SC_MW, SC_OW, SC_AB, SC_OB = range(SCALARS)


def tables():
    p = np.arange(128)
    u = np.arange(-32, 32)
    ang = lambda a, b: 2 * np.pi * ((np.outer(a, b)) % 256) / 256
    fwd = np.zeros((128, HC, 128))
    for a in range(HC):
        h = 2 * p + a
        fwd[:, a, 63:96] = np.cos(ang(h, np.arange(33)))
        fwd[:, a, 96:128] = np.sin(ang(h, np.arange(1, 33)))
    gw = np.zeros((128, WC, 2, 2, NV))
    for c in range(WC):
        w = c * 128 + p
        co, si = np.cos(ang(w, np.arange(NV))), np.sin(ang(w, np.arange(NV)))
        gw[:, c, 0, 0], gw[:, c, 0, 1] = co, -si
        gw[:, c, 1, 0], gw[:, c, 1, 1] = -si, -co
    gw /= H * W
    h = np.concatenate([2 * p, 2 * p + 1])
    inv_h = np.concatenate([np.cos(ang(u, h)), -np.sin(ang(u, h))])
    inv_w = np.zeros((2, 2, NV, 2, W))
    v, w = np.arange(NV), np.arange(W)
    both = np.where(v == 0, 1, 2)[:, None]
    for i in range(2):
        inv_w[i, 0, :, i] = both * np.cos(ang(v, w))
        inv_w[i, 1, :, i] = -both * np.sin(ang(v, w))
    lu = np.concatenate([np.arange(9), np.arange(-8, 0)])
    low_row = (lu[:, None] == u[None, :])
    group_of = (p[:, None] // GW == np.arange(16)[None, :])
    halves = np.stack([p < 64, p >= 64], 1)
    f = lambda t: np.ascontiguousarray(t.reshape(t.shape[0], -1).astype(np.float32))
    return {"t_fwd": f(fwd), "t_w": f(gw), "t_inv_h": f(inv_h), "t_inv_w": f(inv_w.reshape(128, 2 * W)),
            "t_low_row": f(low_row), "t_group": f(group_of), "t_halves": f(halves), "t_eye": f(np.eye(IMGS)),
            "t_pick": f(np.tile(np.arange(2 * IMGS - 1) == IMGS - 1, (128, 1)))}


def spectral_block(nc, x, mix_re, mix_im, mix_mirror, low_w, scalars,
                   t_fwd, t_w, t_inv_h, t_inv_w, t_low_row, t_group, t_halves, t_eye, t_pick, out):
    F32 = mybir.dt.float32
    ALU = mybir.AluOpType
    ACT = mybir.ActivationFunctionType
    AX = mybir.AxisListType
    MUL, ADD, SUB = ALU.mult, ALU.add, ALU.subtract

    ctx = ExitStack()
    with ctx:
        def sb(name, shape):
            return ctx.enter_context(nc.sbuf_tensor(name, shape, F32))

        def sem(name):
            return ctx.enter_context(nc.semaphore(name))

        X = sb("X", [128, IMGS, HC, W])
        Y = sb("Y", [128, IMGS, WC, YC])
        YS = sb("YS", [128, 2, HALF, WC, 2, NU])
        SQ = sb("SQ", [128, 2, HC * W])
        QP = sb("QP", [128, 4, GROUPS])
        FWD = sb("FWD", [128, HC, 128])
        GWT = sb("GWT", [128, WC, 2, 2 * NV])
        GWR = sb("GWR", [128, WC, 2, 2 * NV])
        INVH = sb("INVH", [128, 2 * 128])
        INVW = sb("INVW", [128, 2 * W])
        LOWROW = sb("LOWROW", [128, NU])
        GROUP = sb("GROUP", [128, 16])
        HALVES = sb("HALVES", [128, 2])
        EYE = sb("EYE", [IMGS, IMGS])
        PICK = sb("PICK", [128, 2 * IMGS - 1])
        ONES = sb("ONES", [128, 128])
        SC = sb("SC", [128, SCALARS])
        KK = sb("KK", [128, 6])
        MIXA = sb("MIXA", [NU, 2, NV])
        MIXB = sb("MIXB", [NU, 2, NV])
        OMEGA = sb("OMEGA", [128, 2, NV])
        LWAU = sb("LWAU", [128, IMGS * 2 * LV])
        LW = LWAU[0:IMGS, 0:3 * 2 * LOW].rearrange("p (n r k) -> p n r k", n=3, r=2)
        AU = LWAU[64:64 + LU, :].rearrange("p (i r v) -> p i r v", r=2, v=LV)
        P1 = sb("P1", [NU, G * 2 * NV])
        LO = sb("LO", [NU, G * 2 * LV])
        POW = sb("POW", [128, G * 2 * NV])
        FP = sb("FP", [128, G])
        FM = sb("FM", [128, 2, G])
        CH = sb("CH", [128, 9, G])
        CST = sb("CST", [128, G, 2])
        ALPHA = sb("ALPHA", [128, G, GROUPS])
        S4 = sb("S4", [128, 2, G, 2 * NV])
        T = sb("T", [128, 2, W])
        STA = sb("STA", [IMGS, 64])
        MR = sb("MR", [128, 6, 34])
        IM = sb("IM", [IMGS, 24])
        CB = sb("CB", [128, 3, IMGS])
        A2Q = sb("A2Q", [128, 2, IMGS])
        low3 = lambda ap: ap.rearrange("p (r n) -> p r n", r=2)
        s4f = S4[0:IMGS, :, :, :].rearrange("p a i n -> p (a i n)")
        sqf = SQ[0:IMGS, :, :].rearrange("p a n -> p (a n)")
        QKV = s4f[:, 0:3 * 2 * LOW].rearrange("p (n r k) -> p n r k", n=3, r=2)
        XL = low3(sqf[:, 0:2 * LOW])
        AT = low3(sqf[:, 2 * LOW:4 * LOW])
        PR = sqf[:, 4 * LOW:4 * LOW + 3 * IMGS].rearrange("p (n i) -> p n i", n=3)
        QT = T[:, :, :].rearrange("p a n -> p (a n)").rearrange("p (n i) -> p n i", n=8)
        MRE, MIM, MMIR = P1[:, 0:NV], P1[:, NV:2 * NV], P1[:, 2 * NV:2 * NV + 2]

        def bank(name):
            return ctx.enter_context(nc.psum_tensor(name, [128, 512], F32))
        psY = [bank(f"psY{i}") for i in range(2)]
        psX = bank("psX")
        psT = [bank(f"psT{i}") for i in range(2)]
        psP = [bank(f"psP{i}") for i in range(2)]
        psB = bank("psB")
        psZ = [psP[0], psP[1], psT[0]]

        load_done = [sem(f"load_done{q}") for q in range(NQ)]
        store_done = [sem(f"store_done{q}") for q in range(NQ)]
        tables_in = sem("tables_in")
        setup_vec = sem("setup_vec")
        setup_done = sem("setup_done")
        y_made = sem("y_made")
        y_kept = sem("y_kept")
        rows_made = sem("rows_made")
        half_used = sem("half_used")
        squared = sem("squared")
        q_summed = sem("q_summed")
        q_added = sem("q_added")
        powers = sem("powers")
        products = sem("products")
        powers_weighted = sem("powers_weighted")
        energy_part = sem("energy_part")
        energy_sum = sem("energy_sum")
        energy_kept = sem("energy_kept")
        var_made = sem("var_made")
        root_made = sem("root_made")
        alpha_made = sem("alpha_made")
        s_made = sem("s_made")
        t_made = sem("t_made")
        t_kept = sem("t_kept")
        synth_made = sem("synth_made")
        x_scaled = sem("x_scaled")
        out_made = sem("out_made")
        link = sem("link")
        sums_made = sem("sums_made")
        sums_kept = sem("sums_kept")
        totals_made = sem("totals_made")
        gvar_made = sem("gvar_made")
        groot_made = sem("groot_made")
        scaled_w = sem("scaled_w")
        z_made = sem("z_made")
        ivar_made = sem("ivar_made")
        iroot_made = sem("iroot_made")
        qk_ready = sem("qk_ready")
        qk_turned = sem("qk_turned")
        qk_kept = sem("qk_kept")
        logits_made = sem("logits_made")
        max_made = sem("max_made")
        exp_made = sem("exp_made")
        probs_made = sem("probs_made")
        probs_turned = sem("probs_turned")
        probs_kept = sem("probs_kept")
        att_made = sem("att_made")
        au_made = sem("au_made")
        au_kept = sem("au_kept")
        diag_made = sem("diag_made")
        cb_made = sem("cb_made")
        cb_kept = sem("cb_kept")

        def over(ap, dims):
            return bass.AP(ap.tensor, ap.offset, [list(ap.ap[0])] + dims)

        x_v = x.rearrange("b c (p a) w -> b p c (a w)", a=HC)
        out_v = out.rearrange("b c (p a) w -> b p c (a w)", a=HC)
        Xf = X[:, :, :, :].rearrange("p i a w -> p i (a w)")

        block = ctx.enter_context(nc.Block())

        @block.sync
        def _(sp):
            def load(nb, q):
                sp.dma_start(Xf[:, CHUNK * q:CHUNK * (q + 1), :],
                             x_v[nb, :, CHUNK * q:CHUNK * (q + 1), :]).then_inc(load_done[q], 16)

            def store(b, q):
                sp.wait_ge(out_made, 64 * b + 4 * (q + 1))
                sp.dma_start(out_v[b, :, CHUNK * q:CHUNK * (q + 1), :],
                             Xf[:, CHUNK * q:CHUNK * (q + 1), :]).then_inc(store_done[q], 16)

            small = [(FWD[:, :, :].rearrange("p a n -> p (a n)"), t_fwd),
                     (GWT[:, :, :, :].rearrange("p a b n -> p (a b n)"), t_w), (INVH[:, :], t_inv_h),
                     (INVW[:, :], t_inv_w), (LOWROW[64:64 + LU, :], t_low_row), (GROUP[:, :], t_group),
                     (HALVES[:, :], t_halves), (EYE[:, :], t_eye), (PICK[:, :], t_pick), (SC[:, :], scalars),
                     (MRE, mix_re), (MIM, mix_im), (MMIR, mix_mirror),
                     (LWAU[0:IMGS, 0:3 * 2 * LOW], low_w)]
            sp.dma_start(small[0][0], small[0][1]).then_inc(tables_in, 16)
            load(0, 0)
            for dst, src in small[1:]:
                sp.dma_start(dst, src).then_inc(tables_in, 16)
            for q in range(1, NQ):
                load(0, q)

            def batch(b, more):
                for q in range(NQ):
                    store(b, q)
                    if more:
                        sp.wait_ge(store_done[q], 16 * b + 16)
                        load(b + 1, q)

            batch(0, True)
            with sp.Fori(1, B - 1) as b:
                batch(b, True)
            batch(B - 1, False)
            for q in range(NQ):
                sp.wait_ge(store_done[q], 16 * B)

        @block.tensor
        def _(pe):
            mm = nc.tensor.matmul

            def forward(nb, p):
                if p % 2 == 0:
                    pe.wait_ge(load_done[p // 2], 16 * nb + 16)
                if not (isinstance(nb, int) and nb == 0 and p < 2):
                    pe.wait_ge(y_kept, 32 * nb + p - 1)
                for i in range(2):
                    for c in range(WC):
                        for a in range(HC):
                            last = mm(psY[p % 2][:, (2 * i + c) * 128:(2 * i + c + 1) * 128],
                                      X[:, 2 * p + i, a, c * 128:(c + 1) * 128], FWD[:, a, :],
                                      start=a == 0, stop=a == HC - 1)
                last.then_inc(y_made, 1)

            def add_squares(nb, p):
                pe.wait_ge(q_summed, 64 * nb + 2 * p + 2)
                for i in range(2):
                    n = 2 * p + i
                    last = mm(psB[0:IMGS, 32:64], PICK[:, IMGS - 1 - n:2 * IMGS - 1 - n], QP[:, n % 4, :],
                              start=n == 0, stop=n == IMGS - 1)
                last.then_inc(q_added, 1)

            def modes(b, g):
                pe.wait_ge(energy_kept, 8 * b + g)
                if g == 0:
                    pe.wait_ge(au_kept, 2 * b + 2)
                low = psX[0:NU, :].rearrange("p (i r v) -> p i r v", i=G, r=2)[:, :, :, 0:LV]
                mm(low, LOWROW[64:64 + LU, :], AU[:, G * g:G * (g + 1), :, :], start=True, stop=False,
                   skip_group_check=True)
                for n in range(2):
                    pe.wait_ge(rows_made, 16 * b + 2 * g + n + 1)
                    for i in range(HALF):
                        col = 64 * (HALF * n + i)
                        for c in range(WC):
                            for k in range(2):
                                last = mm(psX[0:NU, col:col + 64], YS[:, n, i, c, k, :], GWR[:, c, k, :],
                                          start=False, stop=(n, i, c, k) == (1, HALF - 1, WC - 1, 1),
                                          skip_group_check=True)
                    last.then_inc(half_used, 1)

            def energy(b, g):
                pe.wait_ge(energy_part, 8 * b + g + 1)
                mm(psX[0:NU, 128:256], LOWROW[64:64 + LU, :],
                   AU[:, G * g:G * (g + 1), :, :].rearrange("p i r v -> p (i r v)"), start=True, stop=True)
                mm(psX[:, 0:2 * G], ONES[:, :], FM[:, :, :].rearrange("p a i -> p (a i)"),
                   start=True, stop=True).then_inc(energy_sum, 1)

            def inverse_h(b, n):
                g, j = divmod(n, PG)
                if j == 0:
                    pe.wait_ge(s_made, 8 * b + g + 1)
                pe.wait_ge(t_kept, 32 * b + max(n - 1, 0))
                mm(psT[n % 2][:, 0:2 * 128],
                   S4[:, g % 2, 2 * j:2 * j + 2, :].rearrange("p i n -> p (i n)"), INVH[:, :],
                   start=True, stop=True).then_inc(t_made, 1)

            def inverse_w(b, n):
                pe.wait_ge(t_kept, 32 * b + n + 1)
                for a in range(HC):
                    pe.wait_ge(out_made, 64 * b + max(2 * n + a - 1, 0))
                    mm(psP[a][:, :], T[:, n % 2, 128 * a:128 * (a + 1)], INVW[:, :],
                       start=True, stop=True).then_inc(synth_made, 1)

            def wait_alone(semaphore, count):
                pe.wait_ge(semaphore, count)
                mm(psY[0][:, 0:1], ONES[0:64, :], ONES[0:64, 0:1], start=True, stop=True)

            def attend(b):
                wait_alone(y_kept, 32 * b + 32)
                for c in range(WC):
                    last = mm(psB[0:IMGS, 16 * c:16 * (c + 1)], Y[:, :, c, 0], GROUP[:, :], start=True, stop=True)
                last.then_inc(sums_made, 1)
                wait_alone(sums_kept, b + 1)
                mm(psB[:, 64:128], ONES[0:IMGS, :], STA[:, :], start=True, stop=True)
                for n in range(2):
                    for c in range(WC):
                        last = mm(psB[:, 128 + 2 * n + c:129 + 2 * n + c],
                                  s4f[:, 256 * n + 128 * c:256 * n + 128 * (c + 1)], ONES[0:IMGS, 0:1],
                                  start=True, stop=True)
                last.then_inc(totals_made, 1)
                wait_alone(scaled_w, b + 1)
                for n in range(LU):
                    col = n if n < 9 else 33 + n - 9
                    for c in range(WC):
                        last = mm(psZ[n // 8][0:IMGS, 64 * (n % 8):64 * (n % 8 + 1)], Y[:, :, c, col],
                                  GWR[:, c, 0, :], start=c == 0, stop=c == WC - 1)
                last.then_inc(z_made, 1)
                wait_alone(qk_ready, b + 1)
                for n in range(8):
                    o, size = (72, 64) if n // 4 else (0, 72)
                    src = QKV[:, (n % 4) // 2, n % 2, o:o + size]
                    last = nc.tensor.transpose(psP[0][0:size, 64 * n:64 * (n + 1)], src, EYE[:, :])
                last.then_inc(qk_turned, 1)
                wait_alone(qk_kept, 2 * b + 2)
                for n in range(4):
                    size, q, k = ((72, n, 2 + n), (64, 2 + n, 4 + n))[n // 2]
                    last = mm(psB[0:IMGS, 256:320], QT[0:size, q, :], QT[0:size, k, :], start=n == 0, stop=n == 3)
                last.then_inc(logits_made, 1)
                wait_alone(probs_made, 2 * b + 1)
                nc.tensor.transpose(psB[0:IMGS, 320:384], PR[:, 0, :], EYE[:, :]).then_inc(probs_turned, 1)
                wait_alone(probs_kept, 2 * b + 1)
                mm(psP[1][0:IMGS, 0:2 * LOW], PR[:, 2, :], QKV[:, 2, :, :].rearrange("p r n -> p (r n)"),
                   start=True, stop=True).then_inc(att_made, 1)
                wait_alone(probs_made, 2 * b + 2)
                nc.tensor.transpose(psB[0:IMGS, 320:384], PR[:, 1, :], EYE[:, :]).then_inc(probs_turned, 1)
                wait_alone(probs_kept, 2 * b + 2)
                for r in range(2):
                    for v in range(LV):
                        vals = QKV[:, 2, r, :].rearrange("p (u v) -> p u v", v=LV)[:, :, v]
                        last = mm(psP[r][0:LU, 64 * v:64 * (v + 1)], vals, PR[:, 2, :], start=True, stop=True)
                last.then_inc(au_made, 1)
                wait_alone(diag_made, b + 1)
                mm(psB[:, 0:3 * IMGS], ONES[0:IMGS, :], P1[0:IMGS, 0:3 * IMGS], start=True, stop=True)\
                    .then_inc(cb_made, 1)

            def produce(b, more):
                for g in range(NG + (LAG if more else 1)):
                    if g < NG:
                        modes(b, g)
                    old, new = 1 <= g <= NG, more and LAG <= g
                    if old:
                        inverse_h(b, PG * (g - 1))
                    for j in range(PG):
                        if old and j < PG - 1:
                            inverse_h(b, PG * (g - 1) + j + 1)
                        if new:
                            forward(b + 1, PG * (g - LAG) + j)
                            if j:
                                add_squares(b + 1, PG * (g - LAG) + j - 1)
                        if old:
                            inverse_w(b, PG * (g - 1) + j)
                        if g < NG and j == PG - 2:
                            energy(b, g)
                    if new:
                        add_squares(b + 1, PG * (g - LAG + 1) - 1)

            pe.wait_ge(tables_in, 16 * 14)
            pe.wait_ge(setup_done, 1)
            for p in range(PAIRS):
                forward(0, p)
                if p:
                    add_squares(0, p - 1)
            add_squares(0, PAIRS - 1)
            attend(0)
            produce(0, True)
            with pe.Fori(1, B - 1) as b:
                attend(b)
                produce(b, True)
            attend(B - 1)
            produce(B - 1, False)

        @block.scalar
        def _(act):
            def keep_y(nb, p):
                act.wait_ge(y_made, 32 * nb + p + 1)
                if not (isinstance(nb, int) and nb == 0):
                    act.wait_ge(half_used, 16 * nb - 16 + 2 * (p // PG) + 2)
                nc.scalar.activation(Y[:, 2 * p:2 * p + 2, :, :].rearrange("p i c n -> p (i c) n"),
                                     psY[p % 2][:, :].rearrange("p (n k) -> p n k", k=128)[:, :, 128 - YC:128],
                                     ACT.Copy).then_inc(y_kept, 1)

            def square(nb, p):
                if p % 2 == 0:
                    act.wait_ge(load_done[p // 2], 16 * nb + 16)
                for n in (2 * p, 2 * p + 1):
                    if not (isinstance(nb, int) and nb == 0 and n < 2):
                        act.wait_ge(q_summed, 64 * nb + n - 1)
                    nc.scalar.activation(SQ[:, n % 2, :], Xf[:, n, :], ACT.Square).then_inc(squared, 1)

            def mode_rows(b, g, halves):
                for n in halves:
                    act.wait_ge(half_used, 16 * b + max(2 * g + n - 1, 0))
                    i0 = G * g + HALF * n
                    y = Y[:, i0:i0 + HALF, :, :].rearrange("p i c k -> p (i c) k")
                    ys = YS[:, n, :, :, :, :].rearrange("p i c k u -> p (i c) k u")
                    nc.scalar.activation(ys[:, :, 0, 0:32], y[:, :, 32:0:-1], ACT.Copy)
                    nc.scalar.activation(ys[:, :, 0, 32:64], y[:, :, 0:32], ACT.Copy)
                    nc.scalar.activation(ys[:, :, 1, 0:32], y[:, :, 64:32:-1], ACT.Copy, scale=-1.0)
                    nc.scalar.activation(ys[:, :, 1, 33:64], y[:, :, 33:64], ACT.Copy).then_inc(rows_made, 1)

            def mode_powers(b, g):
                act.wait_ge(half_used, 16 * b + 2 * g + 2)
                act.wait_ge(energy_part, 8 * b + g)
                for n in range(2):
                    nc.scalar.activation(POW[64 * n:64 * (n + 1), :], psX[0:NU, :], ACT.Square)\
                        .then_inc(powers, 1)

            def keep_t(b, n):
                act.wait_ge(t_made, 32 * b + n + 1)
                act.wait_ge(synth_made, 64 * b + max(2 * n - 2, 0))
                nc.scalar.activation(T[:, n % 2, :], psT[n % 2][:, 0:2 * 128], ACT.Copy)\
                    .then_inc(t_kept, 1)

            def root(b, g):
                act.wait_ge(var_made, 8 * b + g + 1)
                nc.scalar.activation(CH[:, 6, :], CH[:, 5, :], ACT.Sqrt).then_inc(root_made, 1)

            def attend(b):
                act.wait_ge(gvar_made, b + 1)
                nc.scalar.activation(MR[:, 4, :], MR[:, 3, :], ACT.Sqrt).then_inc(groot_made, 1)
                act.wait_ge(ivar_made, 3 * b + 1)
                nc.scalar.activation(IM[:, 5:6], IM[:, 4:5], ACT.Sqrt).then_inc(iroot_made, 1)
                act.wait_ge(qk_turned, b + 1)
                for n in range(2):
                    size = (72, 64)[n]
                    nc.scalar.activation(QT[0:size, 4 * n:4 * n + 4, :].rearrange("p n i -> p (n i)"),
                                         psP[0][0:size, 256 * n:256 * (n + 1)], ACT.Copy).then_inc(qk_kept, 1)
                act.wait_ge(max_made, b + 1)
                nc.scalar.activation(PR[:, 0, :], psB[0:IMGS, 256:320], ACT.Exp, bias=IM[:, 8:9],
                                     scale=LOGIT_SCALE, accum_out=IM[:, 9:10]).then_inc(exp_made, 1)
                for n in range(2):
                    act.wait_ge(probs_turned, 2 * b + n + 1)
                    nc.scalar.activation(PR[:, 2, :], psB[0:IMGS, 320:384], ACT.Copy).then_inc(probs_kept, 1)
                    if n == 0:
                        for m in range(2):
                            act.wait_ge(ivar_made, 3 * b + 2 + m)
                            nc.scalar.activation(IM[:, 5:6], IM[:, 4:5], ACT.Sqrt).then_inc(iroot_made, 1)
                act.wait_ge(au_made, b + 1)
                for r in range(2):
                    nc.scalar.activation(AU[:, :, r, :], psP[r][0:LU, :].rearrange("p (v i) -> p i v", v=LV),
                                         ACT.Copy).then_inc(au_kept, 1)
                act.wait_ge(cb_made, b + 1)
                nc.scalar.activation(CB[:, :, :].rearrange("p n i -> p (n i)"), psB[:, 0:3 * IMGS], ACT.Copy)\
                    .then_inc(cb_kept, 1)

            def produce(b, more):
                for g in range(NG + (LAG if more else 1)):
                    if g < NG:
                        if g == 0:
                            mode_rows(b, 0, (0, 1))
                        mode_powers(b, g)
                    old, new = 1 <= g <= NG, more and LAG <= g
                    if old:
                        keep_t(b, PG * (g - 1))
                    for j in range(PG):
                        if old and j < PG - 1:
                            keep_t(b, PG * (g - 1) + j + 1)
                        if g < NG - 1 and j in (1, 2):
                            mode_rows(b, g + 1, (j - 1,))
                        if new:
                            square(b + 1, PG * (g - LAG) + j)
                            keep_y(b + 1, PG * (g - LAG) + j)
                    if g < NG:
                        root(b, g)

            act.wait_ge(setup_done, 1)
            for p in range(PAIRS):
                square(0, p)
                keep_y(0, p)
            attend(0)
            produce(0, True)
            with act.Fori(1, B - 1) as b:
                attend(b)
                produce(b, True)
            attend(B - 1)
            produce(B - 1, False)


        @block.gpsimd
        def _(pool):
            def weigh(b, g):
                pool.wait_ge(powers, 16 * b + 2 * g + 2)
                v = POW[:, :].rearrange("p (i n) -> p i n", i=G)
                nc.gpsimd.tensor_tensor(v, v, over(OMEGA[:, 0, 0:1], [[0, G], [1, 2 * NV]]), MUL)\
                    .then_inc(powers_weighted, 1)

            def scale_x(b, i):
                if i % G == 0:
                    pool.wait_ge(alpha_made, 8 * b + i // G + 1)
                v = X[:, i, :, :].rearrange("p a (g j) -> p a g j", j=GW)
                al = over(ALPHA[:, i % G, 0:1], [[0, HC], [1, GROUPS], [0, GW]])
                nc.gpsimd.tensor_tensor(v, v, al, MUL).then_inc(x_scaled, 1)

            def produce(b):
                for g in range(NG + 1):
                    if g < NG:
                        weigh(b, g)
                    if g:
                        for i in range(G):
                            scale_x(b, G * (g - 1) + i)

            pool.wait_ge(setup_done, 1)
            produce(0)
            with pool.Fori(1, B) as b:
                produce(b)

        @block.vector
        def _(dve):
            V = nc.vector
            LINKS = 258

            class Chain:
                base, n = 0, 0

            def wait_link():
                dve.wait_ge(link, Chain.base + Chain.n)

            def do(ins):
                ins.then_inc(link, 1)
                Chain.n += 1

            def step(ins):
                do(ins)
                wait_link()

            def tt(out, a, b, op):
                return V.tensor_tensor(out, a, b, op)

            def ts(out, a, s1, s2, op0, op1=None):
                return V.tensor_scalar(out, a, s1, s2, op0) if op1 is None else \
                    V.tensor_scalar(out, a, s1, s2, op0, op1)

            n_setup = [0]

            def setup(ins):
                ins.then_inc(setup_vec, 1)
                n_setup[0] += 1
                dve.wait_ge(setup_vec, n_setup[0])

            setup(V.memset(ONES[:, :], 1.0))
            setup(V.memset(S4[:, :, :, :], 0.0))
            setup(V.memset(YS[:, :, :, :, :, :], 0.0))
            dve.wait_ge(tables_in, 16 * 14)
            setup(V.tensor_copy(MIXA[:, 0, :], MRE))
            setup(V.tensor_copy(MIXA[:, 1, :], MRE))
            setup(V.tensor_copy(MIXB[:, 1, :], MIM))
            setup(V.memset(MIXA[32:33, :, 0:1], 0.0))
            setup(V.memset(MIXB[32:33, 1:2, 0:1], 0.0))
            setup(ts(MIXB[:, 0, :], MIXB[:, 1, :], -1.0, None, MUL))
            w2, w3 = P1[:, 3 * NV:4 * NV], P1[:, 4 * NV:5 * NV]
            setup(tt(w2, MIXA[:, 0, :], MIXA[:, 0, :], MUL))
            setup(tt(w3, MIXB[:, 1, :], MIXB[:, 1, :], MUL))
            setup(tt(w2, w2, w3, ADD))
            setup(ts(OMEGA[0:NU, 0, :], w2, 2.0, None, MUL))
            setup(tt(w3[:, 0:1], MIXA[:, 0, 0:1], MMIR[:, 0:1], MUL))
            setup(tt(w3[:, 1:2], MIXB[:, 1, 0:1], MMIR[:, 1:2], MUL))
            setup(tt(w3[:, 0:1], w3[:, 0:1], w3[:, 1:2], SUB))
            setup(tt(w3[:, 0:1], w3[:, 0:1], w2[:, 0:1], ADD))
            setup(ts(OMEGA[0:NU, 0, 0:1], w3[:, 0:1], 0.5, None, MUL))
            setup(V.tensor_copy(OMEGA[0:NU, 1, :], OMEGA[0:NU, 0, :]))
            setup(ts(OMEGA[64:128, 0, :], MIXA[:, 0, :], 2.0, None, MUL))
            setup(V.tensor_copy(OMEGA[64:128, 0, 0:1], MIXA[:, 0, 0:1]))
            setup(V.tensor_copy(OMEGA[64:128, 1, :], OMEGA[64:128, 0, :]))
            k, mw = SC[:, SC_K:SC_K + 1], SC[:, SC_MW:SC_MW + 1]
            setup(ts(KK[:, 0:1], k, 2.0, None, MUL))
            setup(tt(KK[:, 1:2], k, k, MUL))
            setup(ts(KK[:, 2:3], k, -1.0, None, MUL))
            setup(tt(KK[:, 3:4], mw, mw, MUL))
            setup(ts(KK[:, 3:4], KK[:, 3:4], EPS, None, ADD))
            setup(tt(KK[:, 4:5], mw, SC[:, SC_OW:SC_OW + 1], MUL))
            tt(KK[:, 5:6], SC[:, SC_AB:SC_AB + 1], SC[:, SC_OB:SC_OB + 1], ADD).then_inc(setup_done, 1)
            dve.wait_ge(setup_done, 1)

            def sum_squares(nb, p):
                if not (isinstance(nb, int) and nb == 0 and p < 2):
                    dve.wait_ge(q_added, 32 * nb + p - 1)
                for n in (2 * p, 2 * p + 1):
                    dve.wait_ge(squared, 64 * nb + n + 1)
                    src = SQ[:, n % 2, :].rearrange("p (a g j) -> p g a j", a=HC, j=GW)
                    V.tensor_reduce(QP[:, n % 4, :], src, AX.XY, ADD).then_inc(q_summed, 1)

            def attend(b):
                dve.wait_ge(sums_made, b + 1)
                dve.wait_ge(q_added, 32 * b + 32)
                step(V.tensor_copy(STA[:, :], psB[0:IMGS, 0:64]))
                V.tensor_copy(s4f[:, 0:2 * W].rearrange("p (g j) -> p g j", j=GW),
                              over(STA[:, 0:1], [[1, 64], [0, GW]])).then_inc(sums_kept, 1)
                dve.wait_ge(totals_made, b + 1)
                n_g = 1.0 / (IMGS * H * GW)
                m, q, v, ve, rt, r = (MR[:, n, :] for n in (0, 1, 2, 3, 4, 5))
                for dst in (0, 1):
                    do(ts(MR[:, dst, 0:32], psB[:, 64 + 32 * dst:96 + 32 * dst], n_g, None, MUL))
                    do(ts(MR[:, dst, 32:34], psB[:, 128 + 2 * dst:130 + 2 * dst], n_g, None, MUL))
                wait_link()
                step(tt(v, m, m, MUL))
                step(tt(v, q, v, SUB))
                ts(ve, v, 0.0, EPS, ALU.max, ADD).then_inc(gvar_made, 1)
                dve.wait_ge(groot_made, b + 1)
                step(V.reciprocal(r, rt))
                step(tt(q, r, m, MUL))
                do(ts(v[:, 32:34], m[:, 32:34], float(H), None, MUL))
                wait_link()
                for c in range(WC):
                    do(ts(GWR[:, c, :, :], GWT[:, c, :, :], r[:, 32 + c:33 + c], None, MUL))
                    do(ts(Y[:, :, c, 0], Y[:, :, c, 0], v[:, 32 + c:33 + c], None, SUB))
                for i in range(2):
                    row = INVW[64 * i + NV:64 * i + NV + 1, W * i:W * (i + 1)].rearrange("p (g j) -> p g j", j=GW)
                    src = over(MR[64 * i + NV:64 * i + NV + 1, 1, 0:32], [[1, 32], [0, GW]])
                    do(V.tensor_copy(row, src))
                wait_link()
                V.memset(IM[:, 0:4], 0.0).then_inc(scaled_w, 1)
                S, Q = STA[:, 0:32], STA[:, 32:64]
                t = [P1[0:IMGS, 32 * n:32 * (n + 1)] for n in range(4)]
                mr, rr = MR[0:IMGS, 0, 0:32], MR[0:IMGS, 5, 0:32]
                step(ts(t[0], mr, float(H * GW), None, MUL))
                step(tt(t[0], S, t[0], SUB))
                step(tt(t[1], t[0], rr, MUL))
                do(V.tensor_reduce(IM[:, 0:1], t[1], AX.X, ADD))
                step(tt(t[2], t[0], S, ADD))
                step(tt(t[2], t[2], mr, MUL))
                step(tt(t[2], Q, t[2], SUB))
                step(tt(t[2], t[2], rr, MUL))
                step(tt(t[2], t[2], rr, MUL))
                step(V.tensor_reduce(IM[:, 1:2], t[2], AX.X, ADD))
                step(ts(IM[:, 0:2], IM[:, 0:2], 1.0 / (H * W), None, MUL))
                step(tt(IM[:, 2:3], IM[:, 0:1], IM[:, 0:1], MUL))
                step(tt(IM[:, 2:3], IM[:, 1:2], IM[:, 2:3], SUB))
                ts(IM[:, 4:5], IM[:, 2:3], 0.0, EPS, ALU.max, ADD).then_inc(ivar_made, 1)
                dve.wait_ge(z_made, b + 1)
                Z = P1[0:IMGS, 128:128 + 16 * LU]
                for k in range(3):
                    n = min(8, LU - 8 * k)
                    do(V.tensor_copy(Z[:, 128 * k:128 * k + 16 * n].rearrange("p (n r v) -> p n r v", r=2, v=LV),
                                     psZ[k][0:IMGS, 0:64 * n].rearrange("p (n r v) -> p n r v", r=2, v=NV)
                                     [:, :, :, 0:LV]))
                wait_link()
                Zv = Z.rearrange("p (n r v) -> p n r v", r=2, v=LV)
                Xv = XL[:, :, :].rearrange("p r (u v) -> p r u v", v=LV)
                do(V.tensor_copy(Xv[:, :, 0, :], Zv[:, 0, :, :]))
                co = lambda r: Zv[:, 1:9, r, :]
                si = lambda r: Zv[:, 9:17, r, :]
                do(tt(Xv[:, 0, 1:9, :], co(0), si(1), ADD))
                do(tt(Xv[:, 1, 1:9, :], co(1), si(0), SUB))
                do(tt(Xv[:, 0, 16:8:-1, :], co(0), si(1), SUB))
                do(tt(Xv[:, 1, 16:8:-1, :], co(1), si(0), ADD))
                dve.wait_ge(iroot_made, 3 * b + 1)
                step(V.reciprocal(IM[:, 6:7], IM[:, 5:6]))
                step(tt(IM[:, 6:7], IM[:, 6:7], SC[0:IMGS, SC_N1W:SC_N1W + 1], MUL))
                step(ts(AT[:, :, :], XL[:, :, :], IM[:, 6:7], None, MUL))
                do(V.tensor_copy(AT[:, 0, 0:1], SC[0:IMGS, SC_N1B:SC_N1B + 1]))
                step(V.memset(AT[:, 1, 0:1], 0.0))
                q_t = [POW[0:IMGS, 0:2 * LOW], P1[0:IMGS, 0:2 * LOW], sqf[:, 1024 - 2 * LOW:1024]]
                for n in range(3):
                    for r in range(2):
                        do(tt(QKV[:, n, r, :], LW[:, n, 0, :], AT[:, r, :], MUL))
                        do(tt(low3(q_t[n])[:, r, :], LW[:, n, 1, :], AT[:, 1 - r, :], MUL))
                wait_link()
                for n in range(3):
                    do(tt(QKV[:, n, 0, :], QKV[:, n, 0, :], low3(q_t[n])[:, 0, :], SUB))
                    do(tt(QKV[:, n, 1, :], QKV[:, n, 1, :], low3(q_t[n])[:, 1, :], ADD))
                wait_link()
                kv = QKV[:, 1:3, :, :].rearrange("p n r (u v) -> p n r u v", v=LV)
                e = P1[0:IMGS, 0:64].rearrange("p (n r u) -> p n r u", n=2, r=2)
                for r in range(2):
                    do(tt(e[:, :, r, :], kv[:, :, r, 1:17, 0], kv[:, :, r, 16:0:-1, 0], SUB if r else ADD))
                wait_link()
                for r in range(2):
                    do(ts(kv[:, :, r, 1:17, 0], e[:, :, r, :], 0.5, None, MUL))
                do(V.memset(kv[:, :, 1, 0, 0], 0.0))
                do(V.memset(QKV[:, 2, 0, 0:1], 0.0))
                wait_link()
                twice = QKV[:, 1, :, :].rearrange("p r (u v) -> p (r u) v", v=LV)[:, :, 1:LV]
                ts(twice, twice, 2.0, None, MUL).then_inc(qk_ready, 1)
                dve.wait_ge(logits_made, b + 1)
                step(V.tensor_reduce(IM[:, 7:8], psB[0:IMGS, 256:320], AX.X, ALU.max))
                ts(IM[:, 8:9], IM[:, 7:8], -LOGIT_SCALE, None, MUL).then_inc(max_made, 1)
                dve.wait_ge(exp_made, b + 1)
                step(V.reciprocal(IM[:, 10:11], IM[:, 9:10]))
                ts(PR[:, 0, :], PR[:, 0, :], IM[:, 10:11], None, MUL).then_inc(probs_made, 1)
                dve.wait_ge(att_made, b + 1)
                step(V.tensor_copy(AT[:, :, :].rearrange("p r n -> p (r n)"), psP[1][0:IMGS, 0:2 * LOW]))
                ca, cb = POW[0:IMGS, 0:2 * LOW], P1[0:IMGS, 0:2 * LOW]
                fl = lambda ap: ap.rearrange("p r n -> p (r n)")
                step(ts(ca, fl(AT[:, :, :]), 2.0, None, MUL))
                step(ts(ca[:, ::LV], ca[:, ::LV], 0.5, None, MUL))
                step(tt(cb, ca, fl(XL[:, :, :]), MUL))
                do(V.tensor_reduce(IM[:, 12:13], cb, AX.X, ADD))
                step(tt(ca, ca, fl(AT[:, :, :]), MUL))
                step(V.tensor_reduce(IM[:, 11:12], ca, AX.X, ADD))
                ts(IM[:, 4:5], IM[:, 11:12], EPS, None, ADD).then_inc(ivar_made, 1)
                dve.wait_ge(iroot_made, 3 * b + 2)
                step(V.reciprocal(IM[:, 13:14], IM[:, 5:6]))
                step(tt(IM[:, 13:14], IM[:, 13:14], SC[0:IMGS, SC_AW:SC_AW + 1], MUL))
                ts(PR[:, 1, :], PR[:, 0, :], IM[:, 13:14], None, MUL).then_inc(probs_made, 1)
                step(tt(IM[:, 14:15], IM[:, 11:12], IM[:, 13:14], MUL))
                do(ts(IM[:, 15:16], IM[:, 12:13], 2.0, None, MUL))
                wait_link()
                step(tt(IM[:, 14:15], IM[:, 14:15], IM[:, 15:16], ADD))
                step(tt(IM[:, 14:15], IM[:, 14:15], IM[:, 13:14], MUL))
                step(tt(IM[:, 14:15], IM[:, 14:15], IM[:, 2:3], ADD))
                step(ts(IM[:, 17:18], IM[:, 14:15], 0.0, None, ALU.max))
                ts(IM[:, 4:5], IM[:, 17:18], EPS, None, ADD).then_inc(ivar_made, 1)
                dve.wait_ge(iroot_made, 3 * b + 3)
                step(V.reciprocal(IM[:, 16:17], IM[:, 5:6]))
                step(tt(IM[:, 16:17], IM[:, 16:17], SC[0:IMGS, SC_N2W:SC_N2W + 1], MUL))
                for n, col in enumerate((16, 17, 0)):
                    do(ts(P1[0:IMGS, 64 * n:64 * (n + 1)], EYE[:, :], IM[:, col:col + 1], None, MUL))
                wait_link()
                V.memset(IM[:, 20:21], 0.0).then_inc(diag_made, 1)
                dve.wait_ge(cb_kept, b + 1)
                do(tt(A2Q[:, 0, :], CB[:, 0, :], CB[:, 0, :], MUL))
                do(ts(A2Q[:, 1, :], CB[:, 1, :], KK[:, 1:2], None, MUL))
                wait_link()

            def mix_products(b, g):
                dve.wait_ge(powers, 16 * b + 2 * g + 2)
                src = psX[0:NU, :].rearrange("p (i r v) -> p i r v", i=G, r=2)
                P1v = P1[:, :].rearrange("p (i r v) -> p i r v", i=G, r=2)
                dve.wait_ge(t_made, 32 * b + max(4 * g - 4, 0))
                P2v = S4[0:NU, g % 2, :, :].rearrange("p i (r v) -> p i r v", r=2)
                do(tt(P1v, src, over(MIXA[:, 0, 0:1], [[0, G], [NV, 2], [1, NV]]), MUL))
                wait_link()
                tt(P2v, src[:, :, ::-1, :], over(MIXB[:, 0, 0:1], [[0, G], [NV, 2], [1, NV]]), MUL)\
                    .then_inc(products, 1)

            def energies(b, g):
                dve.wait_ge(powers_weighted, 8 * b + g + 1)
                step(V.tensor_reduce(FP[:, :], POW[:, :].rearrange("p (i n) -> p i n", i=G), AX.X, ADD))
                for n in range(2):
                    ins = ts(FM[:, n, :], FP[:, :], HALVES[:, n:n + 1], None, MUL)
                    if n == 0:
                        do(ins)
                wait_link()
                ins.then_inc(energy_part, 1)
                dve.wait_ge(products, 8 * b + g + 1)
                do(tt(P1[:, :], P1[:, :], S4[0:NU, g % 2, :, :].rearrange("p i n -> p (i n)"), ADD))

            def keep_energies(b, g):
                dve.wait_ge(energy_sum, 8 * b + g + 1)
                do(V.tensor_copy(LO[:, :], psX[0:NU, 128:256]))
                ins = V.tensor_copy(CH[:, 0:2, :].rearrange("p n i -> p (n i)"), psX[:, 0:2 * G])
                wait_link()
                ins.then_inc(energy_kept, 1)
                dve.wait_ge(energy_kept, 8 * b + g + 1)

            def coefficients(b, g):
                i0, i1 = G * g, G * (g + 1)
                c = [CH[:, n + (n > 0), :] for n in range(8)]
                step(V.scalar_tensor_tensor(out=c[1], in0=CH[:, 1, :], scalar=KK[:, 0:1], in1=c[0],
                                            op0=MUL, op1=ADD))
                step(tt(c[2], c[1], A2Q[:, 1, i0:i1], ADD))
                step(V.scalar_tensor_tensor(out=c[3], in0=c[2], scalar=0.0, in1=A2Q[:, 0, i0:i1],
                                            op0=ALU.max, op1=MUL))
                ts(c[4], c[3], KK[:, 3:4], EPS * EPS, MUL, ADD).then_inc(var_made, 1)
                dve.wait_ge(root_made, 8 * b + g + 1)
                step(V.reciprocal(c[6], c[5]))
                step(V.scalar_tensor_tensor(out=c[7], in0=c[6], scalar=KK[:, 4:5], in1=CB[:, 0, i0:i1],
                                            op0=MUL, op1=MUL))
                do(V.scalar_tensor_tensor(out=c[1], in0=c[7], scalar=KK[:, 2:3], in1=CB[:, 2, i0:i1],
                                          op0=MUL, op1=MUL))
                step(ts(c[2], c[7], SC[:, SC_K:SC_K + 1], 1.0, MUL, ADD))
                do(ts(CST[:, :, 0], c[1], KK[:, 5:6], None, ADD))
                do(ts(CST[:, :, 1], c[2], -1.0, None, MUL))
                dve.wait_ge(x_scaled, 64 * b + 8 * g)
                al = ALPHA[:, :, :]
                step(tt(al, over(MR[:, 5, 0:1], [[0, G], [1, GROUPS]]), over(CH[:, 3, 0:1], [[1, G], [0, GROUPS]]),
                        MUL))
                ts(al, al, 1.0, None, ADD).then_inc(alpha_made, 1)
                s = S4[0:NU, g % 2, :, :]
                do(tt(s, P1[:, :].rearrange("p (i n) -> p i n", i=G), over(CH[0:NU, 8, 0:1], [[1, G], [0, 2 * NV]]), MUL))
                lo = LO[:, :].rearrange("p (i n) -> p i n", i=G)
                step(tt(lo, lo,
                        over(CH[0:NU, 3, 0:1], [[1, G], [0, 2 * LV]]), MUL))
                s_lo = s.rearrange("p i (r v) -> p i r v", r=2)[:, :, :, 0:LV]
                step(tt(s_lo, s_lo, lo.rearrange("p i (r v) -> p i r v", r=2), ADD))
                do(V.tensor_copy(S4[64:128, g % 2, :, 0:NV], s[:, :, NV:2 * NV]))
                step(ts(S4[64:128, g % 2, :, NV + 1:2 * NV], s[:, :, 1:NV], -1.0, None, MUL))
                step(V.memset(s[:, :, NV], 0.0))
                row = S4[32:33, g % 2, :, :].rearrange("p i (r v) -> p i r v", r=2)[:, :, :, 0]
                tt(row, row, CST[32:33, :, :], ADD).then_inc(s_made, 1)

            def finish(b, n):
                for a in range(HC):
                    if a == 0:
                        dve.wait_ge(x_scaled, 64 * b + 2 * n + 2)
                    dve.wait_ge(synth_made, 64 * b + 2 * n + a + 1)
                    v = X[:, 2 * n:2 * n + 2, a, :]
                    tt(v, v, psP[a][:, :].rearrange("p (i w) -> p i w", i=2), ADD).then_inc(out_made, 1)

            def produce(b, more):
                for g in range(NG + (LAG if more else 1)):
                    if g < NG:
                        mix_products(b, g)
                    for j in range(PG):
                        if more and LAG <= g:
                            sum_squares(b + 1, PG * (g - LAG) + j)
                        if 1 <= g <= NG:
                            finish(b, PG * (g - 1) + j)
                        if g < NG and j == PG - 3:
                            energies(b, g)
                        if g < NG and j == PG - 2:
                            keep_energies(b, g)
                    if g < NG:
                        coefficients(b, g)

            for p in range(PAIRS):
                sum_squares(0, p)
            attend(0)
            produce(0, True)
            assert Chain.n == LINKS, Chain.n
            with dve.Fori(1, B - 1) as b:
                Chain.base, Chain.n = LINKS * b, 0
                attend(b)
                produce(b, True)
            Chain.base, Chain.n = LINKS * (B - 1), 0
            attend(B - 1)
            produce(B - 1, False)


def kernel(x, L0_conv_kw1, L0_conv_kw2, L0_conv_qw1, L0_conv_qw2, L0_conv_vw1, L0_conv_vw2, L0_conv_mix_w1,
           L0_conv_mix_w2, L0_conv_mix_bias, L0_conv_mix_skip_w, L0_conv_mix_skip_b, L0_conv_mix_norm_w,
           L0_conv_mix_norm_b, L0_conv_norm1_w, L0_conv_norm1_b, L0_conv_an_w, L0_conv_an_b, L0_conv_norm2_w,
           L0_conv_norm2_b, L0_conv_mon_w, L0_conv_mon_b):
    import concourse.bacc as bacc
    from concourse.bass_utils import run_bass_kernel_spmd

    def low(w1, w2):
        w1, w2 = np.asarray(w1)[0, 0], np.asarray(w2)[0, 0]
        rows = np.concatenate([w1, np.zeros((1,) + w1.shape[1:], w1.dtype), w2])
        return rows.transpose(2, 0, 1).reshape(-1)

    low_w = np.concatenate([low(L0_conv_qw1, L0_conv_qw2), low(L0_conv_kw1, L0_conv_kw2),
                            low(L0_conv_vw1, L0_conv_vw2)])
    w1, w2 = np.asarray(L0_conv_mix_w1)[0, 0], np.asarray(L0_conv_mix_w2)[0, 0]
    mix = np.concatenate([w2, w1])
    mirror = np.concatenate([np.zeros_like(mix[:1, 0]), mix[:0:-1, 0]])
    scal = np.concatenate([np.asarray(a).reshape(1) for a in (
        L0_conv_norm1_w, L0_conv_norm1_b, L0_conv_an_w, L0_conv_norm2_w, L0_conv_mix_skip_w,
        L0_conv_mix_norm_w, L0_conv_mon_w, L0_conv_an_b, L0_conv_mon_b)])
    arrays = {
        "in_x": np.ascontiguousarray(x),
        "in_mix_re": np.ascontiguousarray(mix[:, :, 0]), "in_mix_im": np.ascontiguousarray(mix[:, :, 1]),
        "in_mix_mirror": np.ascontiguousarray(mirror),
        "in_low_w": np.ascontiguousarray(np.broadcast_to(low_w, (IMGS, low_w.size))),
        "in_scalars": np.ascontiguousarray(np.broadcast_to(scal, (128, SCALARS))),
        **tables(),
    }
    nc = bacc.Bacc("TRN2", target_bir_lowering=False, num_devices=1)
    args = [nc.dram_tensor(n, a.shape, mybir.dt.from_np(a.dtype), kind="ExternalInput").ap()
            for n, a in arrays.items()]
    out = nc.dram_tensor("out", (B, IMGS, H, W), mybir.dt.float32, kind="ExternalOutput").ap()
    spectral_block(nc, *args, out)
    r = run_bass_kernel_spmd(nc, [arrays], core_ids=[0])
    return r.results[0]["out"]
```

```python
import numpy as np
from contextlib import ExitStack

import concourse.bass as bass
from concourse import mybir

B, IMGS, H, W = 4, 64, 256, 256
GROUPS, GW = 32, 8
HC = WC = 2
NU, NV = 64, 32
LU, LV = 17, 8
LOW = LU * LV
YC = 33 + 32
HALF = 4
G = 8
NG = IMGS // G
PAIRS = IMGS // 2
PG = G // 2
TABLES = 12
LAG = 2
EPS = 1e-5
LOGIT_SCALE = float(64 * 64) * 64.0
SCALARS = 9
SC_N1W, SC_N1B, SC_AW, SC_N2W, SC_K, SC_MW, SC_OW, SC_AB, SC_OB = range(SCALARS)


def tables():
    p = np.arange(128)
    u = np.arange(-32, 32)
    ang = lambda a, b: 2 * np.pi * ((np.outer(a, b)) % 256) / 256
    fwd = np.zeros((128, HC, 128))
    for a in range(HC):
        h = 2 * p + a
        fwd[:, a, 63:96] = np.cos(ang(h, np.arange(33)))
        fwd[:, a, 96:128] = np.sin(ang(h, np.arange(1, 33)))
    gw = np.zeros((128, WC, 2, 2, NV))
    for c in range(WC):
        w = c * 128 + p
        co, si = np.cos(ang(w, np.arange(NV))), np.sin(ang(w, np.arange(NV)))
        gw[:, c, 0, 0], gw[:, c, 0, 1] = co, -si
        gw[:, c, 1, 0], gw[:, c, 1, 1] = -si, -co
    gw /= H * W
    h = np.concatenate([2 * p, 2 * p + 1])
    inv_h = np.concatenate([np.cos(ang(u, h)), -np.sin(ang(u, h))])
    v, w = np.arange(NV), np.arange(W)
    both = np.where(v == 0, 1, 2)[:, None]
    inv_w = np.tile(np.concatenate([both * np.cos(ang(v, w)), -both * np.sin(ang(v, w))]), (2, 1))
    lu = np.concatenate([np.arange(9), np.arange(-8, 0)])
    low_row = (lu[:, None] == u[None, :])
    group_of = (p[:, None] // GW == np.arange(16)[None, :])
    f = lambda t: np.ascontiguousarray(t.reshape(t.shape[0], -1).astype(np.float32))
    return {"t_fwd": f(fwd), "t_w": f(gw), "t_inv_h": f(inv_h), "t_inv_w": f(inv_w),
            "t_low_row": f(low_row), "t_group": f(group_of), "t_eye": f(np.eye(IMGS)),
            "t_pick": f(np.tile(np.arange(2 * IMGS - 1) == IMGS - 1, (128, 1)))}


def spectral_block(nc, x, mix_re, mix_im, mix_mirror, low_w, scalars,
                   t_fwd, t_w, t_inv_h, t_inv_w, t_low_row, t_group, t_eye, t_pick, out):
    F32 = mybir.dt.float32
    F32R = mybir.dt.float32r
    ALU = mybir.AluOpType
    ACT = mybir.ActivationFunctionType
    AX = mybir.AxisListType
    MUL, ADD, SUB = ALU.mult, ALU.add, ALU.subtract

    ctx = ExitStack()
    with ctx:
        def sb(name, shape, dt=F32):
            return ctx.enter_context(nc.sbuf_tensor(name, shape, dt))

        def sem(name):
            return ctx.enter_context(nc.semaphore(name))

        X = sb("X", [128, IMGS, HC, W])
        Y = sb("Y", [128, IMGS, WC, YC])
        YS = sb("YS", [128, 2, HALF, WC, 2, NU])
        SQ = sb("SQ", [128, 4, HC * W])
        QP = sb("QP", [128, 4, GROUPS])
        FWD = sb("FWD", [128, HC, 128])
        GWT = sb("GWT", [128, WC, 2, 2 * NV])
        GWR = sb("GWR", [128, WC, 2, 2 * NV])
        INVH = sb("INVH", [128, 2 * 128])
        INVW = sb("INVW", [128, 2, W], F32R)
        LOWROW = sb("LOWROW", [128, NU])
        GROUP = sb("GROUP", [128, 16])
        EYE = sb("EYE", [IMGS, IMGS])
        PICK = sb("PICK", [128, 2 * IMGS - 1])
        ONES = sb("ONES", [128, 128])
        SC = sb("SC", [128, SCALARS])
        KK = sb("KK", [128, 6])
        MIXA = sb("MIXA", [NU, 2, NV])
        MIXB = sb("MIXB", [NU, 2, NV])
        OMEGA = sb("OMEGA", [128, 2, NV])
        LWAU = sb("LWAU", [128, IMGS * 2 * LV])
        LW = LWAU[0:IMGS, 0:3 * 2 * LOW].rearrange("p (n r k) -> p n r k", n=3, r=2)
        AU = LWAU[64:64 + LU, :].rearrange("p (i r v) -> p i r v", r=2, v=LV)
        P1 = sb("P1", [NU, G * 2 * NV])
        LO = sb("LO", [NU, G * 2 * LV])
        POW = sb("POW", [128, G * 2 * NV])
        WEIGHTS = sb("WEIGHTS", [128, 128])
        FP = sb("FP", [128, G])
        CH = sb("CH", [128, 9, G])
        CST = sb("CST", [128, G, 2])
        ALPHA = sb("ALPHA", [128, 2, G, GROUPS])
        S4 = sb("S4", [128, 2, G, 2 * NV])
        T = sb("T", [128, 2, 2, 2 * 128], F32R)
        STA = sb("STA", [IMGS, 64])
        MR = sb("MR", [128, 6, GROUPS])
        MW = sb("MW", [128, 3, WC])
        IM = sb("IM", [IMGS, 24])
        CB = sb("CB", [128, 4, IMGS])
        A2Q = sb("A2Q", [128, 2, IMGS])
        low3 = lambda ap: ap.rearrange("p (r n) -> p r n", r=2)
        s4f = S4[0:IMGS, :, :, :].rearrange("p a i n -> p (a i n)")
        sqf = SQ[0:IMGS, :, :].rearrange("p a n -> p (a n)")
        QKV = s4f[:, 0:3 * 2 * LOW].rearrange("p (n r k) -> p n r k", n=3, r=2)
        XL = low3(sqf[:, 0:2 * LOW])
        AT = low3(sqf[:, 2 * LOW:4 * LOW])
        PR = sqf[:, 4 * LOW:4 * LOW + 2 * IMGS].rearrange("p (n i) -> p n i", n=2)
        QKT = sqf[:, 5 * LOW:9 * LOW].rearrange("p (n r k) -> p n r k", n=2, r=2)
        VT = sqf[:, 9 * LOW:11 * LOW].rearrange("p (n r k) -> p n r k", n=1, r=2)
        XL2 = sqf[:, 11 * LOW:13 * LOW]
        QT = POW[:, :].rearrange("p (n i) -> p n i", n=8)
        MRE, MIM, MMIR = P1[:, 0:NV], P1[:, NV:2 * NV], P1[:, 2 * NV:2 * NV + 2]

        def bank(name):
            return ctx.enter_context(nc.psum_tensor(name, [128, 512], F32))
        psY = [bank(f"psY{i}") for i in range(2)]
        psX = bank("psX")
        psT = [bank(f"psT{i}") for i in range(2)]
        psP = [bank(f"psP{i}") for i in range(2)]
        psB = bank("psB")
        psZ = [psP[0], psP[1], psT[0]]

        load_done = [sem(f"load_done{q}") for q in range(PAIRS)]
        store_done = [sem(f"store_done{q}") for q in range(PAIRS)]
        fwd_in = sem("fwd_in")
        tables_in = sem("tables_in")
        setup_vec = sem("setup_vec")
        setup_done = sem("setup_done")
        y_made = sem("y_made")
        y_kept = sem("y_kept")
        rows_made = sem("rows_made")
        half_used = sem("half_used")
        modes_made = sem("modes_made")
        squared = sem("squared")
        folded = sem("folded")
        q_summed = sem("q_summed")
        q_added = sem("q_added")
        powers = sem("powers")
        products = sem("products")
        powers_weighted = sem("powers_weighted")
        energy_part = sem("energy_part")
        energy_sum = sem("energy_sum")
        energy_kept = sem("energy_kept")
        var_made = sem("var_made")
        root_made = sem("root_made")
        alpha_made = sem("alpha_made")
        s_made = sem("s_made")
        t_made = sem("t_made")
        t_high = sem("t_high")
        t_kept = sem("t_kept")
        synth_made = sem("synth_made")
        x_scaled = sem("x_scaled")
        out_made = sem("out_made")
        link = sem("link")
        sums_made = sem("sums_made")
        sums_kept = sem("sums_kept")
        totals_made = sem("totals_made")
        gvar_made = sem("gvar_made")
        groot_made = sem("groot_made")
        scaled_w = sem("scaled_w")
        z_made = sem("z_made")
        ivar_made = sem("ivar_made")
        iroot_made = sem("iroot_made")
        qk_ready = sem("qk_ready")
        qk_turned = sem("qk_turned")
        qk_kept = sem("qk_kept")
        logits_made = sem("logits_made")
        max_made = sem("max_made")
        exp_made = sem("exp_made")
        probs_made = sem("probs_made")
        probs_turned = sem("probs_turned")
        probs_kept = sem("probs_kept")
        att_squared = sem("att_squared")
        att_made = sem("att_made")
        au_made = sem("au_made")
        au_kept = sem("au_kept")
        diag_made = sem("diag_made")
        cb_made = sem("cb_made")
        cb_kept = sem("cb_kept")

        def over(ap, dims):
            return bass.AP(ap.tensor, ap.offset, [list(ap.ap[0])] + dims)

        x_v = x.rearrange("b c (p a) w -> b p c (a w)", a=HC)
        out_v = out.rearrange("b c (p a) w -> b p c (a w)", a=HC)
        Xf = X[:, :, :, :].rearrange("p i a w -> p i (a w)")

        block = ctx.enter_context(nc.Block())

        @block.sync
        def _(sp):
            def load(nb, q):
                sp.dma_start(Xf[:, 2 * q:2 * (q + 1), :],
                             x_v[nb, :, 2 * q:2 * (q + 1), :]).then_inc(load_done[q], 16)

            def store(b, q):
                sp.wait_ge(out_made, 64 * b + 2 * (q + 1))
                sp.dma_start(out_v[b, :, 2 * q:2 * (q + 1), :],
                             Xf[:, 2 * q:2 * (q + 1), :]).then_inc(store_done[q], 16)

            small = [(GWT[:, :, :, :].rearrange("p a b n -> p (a b n)"), t_w), (INVH[:, :], t_inv_h),
                     (POW[:, 0:W], t_inv_w), (LOWROW[64:64 + LU, :], t_low_row), (GROUP[:, :], t_group),
                     (EYE[:, :], t_eye), (PICK[:, :], t_pick), (SC[:, :], scalars),
                     (MRE, mix_re), (MIM, mix_im), (MMIR, mix_mirror),
                     (LWAU[0:IMGS, 0:3 * 2 * LOW], low_w)]
            sp.dma_start(FWD[:, :, :].rearrange("p a n -> p (a n)"), t_fwd).then_inc(fwd_in, 16)
            for q in range(PAIRS):
                load(0, q)
                for dst, src in small[6 * q - 6:6 * q] if q else ():
                    sp.dma_start(dst, src).then_inc(tables_in, 16)

            def batch(b, more):
                for q in range(PAIRS + 1):
                    if q < PAIRS:
                        store(b, q)
                    if more and q:
                        sp.wait_ge(store_done[q - 1], 16 * b + 16)
                        load(b + 1, q - 1)

            batch(0, True)
            with sp.Fori(1, B - 1) as b:
                batch(b, True)
            batch(B - 1, False)
            for q in range(PAIRS):
                sp.wait_ge(store_done[q], 16 * B)

        @block.tensor
        def _(pe):
            mm = nc.tensor.matmul

            def forward(nb, p):
                pe.wait_ge(load_done[p], 16 * nb + 16)
                if not (isinstance(nb, int) and nb == 0 and p < 2):
                    pe.wait_ge(y_kept, 32 * nb + p - 1)
                for i in range(2):
                    for c in range(WC):
                        for a in range(HC):
                            last = mm(psY[p % 2][:, (2 * i + c) * 128:(2 * i + c + 1) * 128],
                                      X[:, 2 * p + i, a, c * 128:(c + 1) * 128], FWD[:, a, :],
                                      start=a == 0, stop=a == HC - 1)
                last.then_inc(y_made, 1)

            def add_squares(nb, p):
                pe.wait_ge(q_summed, 64 * nb + 2 * p + 2)
                for i in range(2):
                    n = 2 * p + i
                    last = mm(psB[0:IMGS, 32:64], PICK[:, IMGS - 1 - n:2 * IMGS - 1 - n], QP[:, n % 4, :],
                              start=n == 0, stop=n == IMGS - 1)
                last.then_inc(q_added, 1)

            def modes(b, g):
                if g == 1:
                    pe.wait_ge(products, 8 * b + 1)
                else:
                    pe.wait_ge(energy_kept, 8 * b + g)
                for n in range(2):
                    pe.wait_ge(rows_made, 16 * b + 2 * g + n + 1)
                    for i in range(HALF):
                        col = 64 * (HALF * n + i)
                        for c in range(WC):
                            for k in range(2):
                                last = mm(psX[0:NU, col:col + 64], YS[:, n, i, c, k, :], GWR[:, c, k, :],
                                          start=(n, i, c, k) == (0, 0, 0, 0), stop=False, skip_group_check=True)
                    last.then_inc(half_used, 1)

            def add_attention(b, g):
                if g < 2:
                    pe.wait_ge(au_kept, 4 * b + 2 * g + 2)
                pe.wait_ge(half_used, 16 * b + 2 * g + 2)
                low = psX[0:NU, :].rearrange("p (i r v) -> p i r v", i=G, r=2)[:, :, :, 0:LV]
                mm(low, LOWROW[64:64 + LU, :], AU[:, G * g:G * (g + 1), :, :], start=False, stop=True,
                   skip_group_check=True).then_inc(modes_made, 1)

            def energy(b, g):
                pe.wait_ge(energy_part, 8 * b + g + 1)
                ps = psX if g else psT[0]
                mm(ps[0:NU, 128:256], LOWROW[64:64 + LU, :],
                   AU[:, G * g:G * (g + 1), :, :].rearrange("p i r v -> p (i r v)"), start=True, stop=True)
                mm(ps[:, 0:G], WEIGHTS[:, :], FP[:, :], start=True, stop=True).then_inc(energy_sum, 1)

            def inverse_h(b, n):
                g, j = divmod(n, PG)
                if j == 0:
                    pe.wait_ge(s_made, 8 * b + g + 1)
                pe.wait_ge(t_kept, 64 * b + max(2 * n - 2, 0))
                mm(psT[n % 2][:, 0:2 * 128],
                   S4[:, g % 2, 2 * j:2 * j + 2, :].rearrange("p i n -> p (i n)"), INVH[:, :],
                   start=True, stop=True).then_inc(t_made, 1)

            def inverse_w(b, n):
                pe.wait_ge(t_kept, 64 * b + 2 * n + 2)
                for a in range(HC):
                    pe.wait_ge(out_made, 64 * b + max(2 * n + a - 1, 0))
                    for i in range(2):
                        for part in range(2):
                            last = mm(psP[a][:, W * i:W * (i + 1)], T[:, n % 2, i, 128 * a:128 * (a + 1)],
                                      INVW[:, part, :], start=part == 0, stop=part == 1)
                    last.then_inc(synth_made, 1)

            def wait_alone(semaphore, count):
                pe.wait_ge(semaphore, count)
                mm(psY[0][:, 0:1], ONES[0:64, :], ONES[0:64, 0:1], start=True, stop=True)

            def attend(b):
                pe.wait_ge(y_kept, 32 * b + 32)
                for c in range(WC):
                    last = mm(psB[0:IMGS, 16 * c:16 * (c + 1)], Y[:, :, c, 0], GROUP[:, :], start=True, stop=True)
                last.then_inc(sums_made, 1)
                pe.wait_ge(sums_kept, b + 1)
                mm(psB[:, 64:128], ONES[0:IMGS, :], STA[:, :], start=True, stop=True).then_inc(totals_made, 1)
                pe.wait_ge(scaled_w, b + 1)
                for n in range(LU):
                    col = n if n < 9 else 33 + n - 9
                    for c in range(WC):
                        last = mm(psZ[n // 8][0:IMGS, 64 * (n % 8):64 * (n % 8 + 1)], Y[:, :, c, col],
                                  GWR[:, c, 0, :], start=c == 0, stop=c == WC - 1)
                last.then_inc(z_made, 1)
                modes(b, 0)
                wait_alone(qk_ready, b + 1)
                for n in range(8):
                    o, size = (72, 64) if n // 4 else (0, 72)
                    src = QKV[:, (n % 4) // 2, n % 2, o:o + size]
                    last = nc.tensor.transpose(psP[0][0:size, 64 * n:64 * (n + 1)], src, EYE[:, :])
                last.then_inc(qk_turned, 1)
                wait_alone(qk_kept, 2 * b + 2)
                for n in range(4):
                    size, q, k = ((72, n, 2 + n), (64, 2 + n, 4 + n))[n // 2]
                    last = mm(psB[0:IMGS, 256:320], QT[0:size, q, :], QT[0:size, k, :], start=n == 0, stop=n == 3)
                last.then_inc(logits_made, 1)
                wait_alone(probs_made, b + 1)
                nc.tensor.transpose(psB[0:IMGS, 320:384], PR[:, 0, :], EYE[:, :]).then_inc(probs_turned, 1)
                wait_alone(probs_kept, b + 1)
                mm(psT[1][0:IMGS, 0:2 * LOW], PR[:, 1, :], QKV[:, 2, :, :].rearrange("p r n -> p (r n)"),
                   start=True, stop=True).then_inc(att_made, 1)
                for r in range(2):
                    for v in range(LV):
                        vals = QKV[:, 2, r, :].rearrange("p (u v) -> p u v", v=LV)[:, :, v]
                        last = mm(psP[r][0:LU, 64 * v:64 * (v + 1)], vals, PR[:, 1, :], start=True, stop=True)
                last.then_inc(au_made, 1)
                pe.wait_ge(diag_made, b + 1)
                mm(psB[:, 0:4 * IMGS], ONES[0:IMGS, :], P1[0:IMGS, 0:4 * IMGS], start=True, stop=True)\
                    .then_inc(cb_made, 1)

            def produce(b, more):
                for g in range(NG + (LAG if more else 1)):
                    old, new, p0, q0 = 1 <= g <= NG, more and LAG <= g, PG * (g - 1), PG * (g - LAG)
                    if g < NG:
                        if g:
                            modes(b, g)
                        add_attention(b, g)
                    if old:
                        inverse_h(b, p0)
                        inverse_h(b, p0 + 1)
                    for j in range(PG):
                        if new:
                            forward(b + 1, q0 + j)
                        if g < NG and j == 1:
                            energy(b, g)
                        if old:
                            inverse_w(b, p0 + j)
                            if j < PG - 2:
                                inverse_h(b, p0 + j + 2)
                        if new and q0 + j >= 2:
                            add_squares(b + 1, q0 + j - 2)
                if more:
                    add_squares(b + 1, PAIRS - 2)
                    add_squares(b + 1, PAIRS - 1)

            pe.wait_ge(fwd_in, 16)
            for p in range(PAIRS):
                forward(0, p)
                if p == 2:
                    pe.wait_ge(tables_in, 16 * TABLES)
                if p >= 2:
                    add_squares(0, p - 2)
            for p in range(PAIRS - 2, PAIRS):
                add_squares(0, p)
            pe.wait_ge(setup_done, 1)
            attend(0)
            produce(0, True)
            with pe.Fori(1, B - 1) as b:
                attend(b)
                produce(b, True)
            attend(B - 1)
            produce(B - 1, False)

        @block.scalar
        def _(act):
            def keep_y(nb, p):
                act.wait_ge(y_made, 32 * nb + p + 1)
                if not (isinstance(nb, int) and nb == 0):
                    act.wait_ge(half_used, 16 * nb - 16 + 2 * (p // PG) + 2)
                nc.scalar.activation(Y[:, 2 * p:2 * p + 2, :, :].rearrange("p i c n -> p (i c) n"),
                                     psY[p % 2][:, :].rearrange("p (n k) -> p n k", k=128)[:, :, 128 - YC:128],
                                     ACT.Copy).then_inc(y_kept, 1)

            def square(nb, p):
                act.wait_ge(load_done[p], 16 * nb + 16)
                for n in (2 * p, 2 * p + 1):
                    if not (isinstance(nb, int) and nb == 0 and n < 4):
                        act.wait_ge(q_summed, 64 * nb + n - 3)
                    nc.scalar.activation(SQ[:, n % 4, :], Xf[:, n, :], ACT.Square).then_inc(squared, 1)

            def mode_rows(b, g, halves):
                for n in halves:
                    act.wait_ge(half_used, 16 * b + max(2 * g + n - 1, 0))
                    i0 = G * g + HALF * n
                    y = Y[:, i0:i0 + HALF, :, :].rearrange("p i c k -> p (i c) k")
                    ys = YS[:, n, :, :, :, :].rearrange("p i c k u -> p (i c) k u")
                    nc.scalar.activation(ys[:, :, 0, 0:32], y[:, :, 32:0:-1], ACT.Copy)
                    nc.scalar.activation(ys[:, :, 0, 32:64], y[:, :, 0:32], ACT.Copy)
                    nc.scalar.activation(ys[:, :, 1, 0:32], y[:, :, 64:32:-1], ACT.Copy, scale=-1.0)
                    nc.scalar.activation(ys[:, :, 1, 33:64], y[:, :, 33:64], ACT.Copy).then_inc(rows_made, 1)

            def mode_powers(b, g):
                act.wait_ge(modes_made, 8 * b + g + 1)
                act.wait_ge(energy_part, 8 * b + g)
                for n in range(2):
                    nc.scalar.activation(POW[64 * n:64 * (n + 1), :], psX[0:NU, :], ACT.Square)\
                        .then_inc(powers, 1)

            def keep_t(b, n):
                act.wait_ge(t_made, 32 * b + n + 1)
                act.wait_ge(synth_made, 64 * b + max(2 * n - 2, 0))
                for i in range(2):
                    rows = slice(64 * i, 64 * (i + 1))
                    nc.scalar.activation(T[rows, n % 2, i, :], psT[n % 2][rows, 0:256], ACT.Copy)\
                        .then_inc(t_high, 1)

            def root(b, g):
                act.wait_ge(var_made, 8 * b + g + 1)
                nc.scalar.activation(CH[:, 6, :], CH[:, 5, :], ACT.Sqrt).then_inc(root_made, 1)

            def attend(b):
                act.wait_ge(gvar_made, b + 1)
                nc.scalar.activation(MR[:, 4, :], MR[:, 3, :], ACT.Sqrt).then_inc(groot_made, 1)
                act.wait_ge(ivar_made, 3 * b + 1)
                nc.scalar.activation(IM[:, 5:6], IM[:, 4:5], ACT.Sqrt).then_inc(iroot_made, 1)
                mode_rows(b, 0, (0, 1))
                act.wait_ge(qk_turned, b + 1)
                for n in range(2):
                    size = (72, 64)[n]
                    nc.scalar.activation(QT[0:size, 4 * n:4 * n + 4, :].rearrange("p n i -> p (n i)"),
                                         psP[0][0:size, 256 * n:256 * (n + 1)], ACT.Copy).then_inc(qk_kept, 1)
                act.wait_ge(max_made, b + 1)
                nc.scalar.activation(PR[:, 0, :], psB[0:IMGS, 256:320], ACT.Exp, bias=IM[:, 8:9],
                                     scale=LOGIT_SCALE, accum_out=IM[:, 9:10]).then_inc(exp_made, 1)
                act.wait_ge(probs_turned, b + 1)
                nc.scalar.activation(PR[:, 1, :], psB[0:IMGS, 320:384], ACT.Copy).then_inc(probs_kept, 1)
                nc.scalar.activation(IM[:, 21:22], IM[:, 20:21], ACT.Sqrt)
                act.wait_ge(att_made, b + 1)
                nc.scalar.activation(POW[0:IMGS, 0:2 * LOW], psT[1][0:IMGS, 0:2 * LOW], ACT.Square,
                                     accum_out=IM[:, 18:19])
                nc.scalar.activation(POW[0:IMGS, 2 * LOW:2 * LOW + 2 * LU], psT[1][0:IMGS, 0:2 * LOW:LV],
                                     ACT.Square, accum_out=IM[:, 19:20]).then_inc(att_squared, 1)
                for m in range(2):
                    act.wait_ge(ivar_made, 3 * b + 2 + m)
                    nc.scalar.activation(IM[:, 5:6], IM[:, 4:5], ACT.Sqrt).then_inc(iroot_made, 1)
                act.wait_ge(cb_made, b + 1)
                nc.scalar.activation(CB[:, :, :].rearrange("p n i -> p (n i)"), psB[:, 0:4 * IMGS], ACT.Copy)\
                    .then_inc(cb_kept, 1)

            def produce(b, more):
                for g in range(NG + (LAG if more else 1)):
                    old, new, p0, q0 = 1 <= g <= NG, more and LAG <= g, PG * (g - 1), PG * (g - LAG)
                    if new:
                        square(b + 1, q0)
                    if old:
                        keep_t(b, p0)
                        keep_t(b, p0 + 1)
                    if g < NG:
                        mode_powers(b, g)
                    for j in range(PG):
                        if new:
                            keep_y(b + 1, q0 + j)
                        if old and j < PG - 2:
                            keep_t(b, p0 + j + 2)
                        if g < NG and j == 2:
                            root(b, g)
                        if new and j < PG - 1:
                            square(b + 1, q0 + j + 1)
                        if g < NG - 1 and j in (0, 2):
                            mode_rows(b, g + 1, (j // 2,))

            for p in range(PAIRS):
                keep_y(0, p)
                square(0, p)
            attend(0)
            produce(0, True)
            with act.Fori(1, B - 1) as b:
                attend(b)
                produce(b, True)
            attend(B - 1)
            produce(B - 1, False)


        @block.gpsimd
        def _(pool):
            def weigh(b, g):
                pool.wait_ge(powers, 16 * b + 2 * g + 2)
                v = POW[:, :].rearrange("p (i n) -> p i n", i=G)
                nc.gpsimd.tensor_tensor(v, v, over(OMEGA[:, 0, 0:1], [[0, G], [1, 2 * NV]]), MUL)\
                    .then_inc(powers_weighted, 1)

            def scale_x(b, i):
                if i % G == 0:
                    pool.wait_ge(alpha_made, 8 * b + i // G + 1)
                v = X[:, i, :, :].rearrange("p a (g j) -> p a g j", j=GW)
                al = over(ALPHA[:, i // G % 2, i % G, 0:1], [[0, HC], [1, GROUPS], [0, GW]])
                nc.gpsimd.tensor_tensor(v, v, al, MUL).then_inc(x_scaled, 1)

            def fold(nb, n):
                pool.wait_ge(squared, 64 * nb + n + 1)
                lo = SQ[:, n % 4, 0:W]
                nc.gpsimd.tensor_tensor(lo, lo, SQ[:, n % 4, W:2 * W], ADD).then_inc(folded, 1)

            def produce(b, more):
                for g in range(NG + (LAG if more else 1)):
                    old, new, i0, n0 = 1 <= g <= NG, more and LAG <= g, G * (g - 1), G * (g - LAG)
                    if old:
                        for i in range(4):
                            scale_x(b, i0 + i)
                    if g < NG:
                        weigh(b, g)
                    for i in range(0, G, 2):
                        if new:
                            fold(b + 1, n0 + i)
                            fold(b + 1, n0 + i + 1)
                        if old and i < G - 4:
                            scale_x(b, i0 + i + 4)
                            scale_x(b, i0 + i + 5)

            for n in range(IMGS):
                fold(0, n)
            produce(0, True)
            with pool.Fori(1, B - 1) as b:
                produce(b, True)
            produce(B - 1, False)

        @block.vector
        def _(dve):
            V = nc.vector
            LINKS = 215

            class Chain:
                base, n = 0, 0

            def wait_link():
                dve.wait_ge(link, Chain.base + Chain.n)

            def do(ins):
                ins.then_inc(link, 1)
                Chain.n += 1

            def step(ins):
                do(ins)
                wait_link()

            def tt(out, a, b, op):
                return V.tensor_tensor(out, a, b, op)

            def ts(out, a, s1, s2, op0, op1=None):
                return V.tensor_scalar(out, a, s1, s2, op0) if op1 is None else \
                    V.tensor_scalar(out, a, s1, s2, op0, op1)

            n_setup = [0]

            def setup(ins):
                ins.then_inc(setup_vec, 1)
                n_setup[0] += 1
                dve.wait_ge(setup_vec, n_setup[0])

            setup(V.memset(ONES[:, :], 1.0))
            setup(V.memset(S4[:, :, :, :], 0.0))
            setup(V.memset(YS[:, :, :, :, :, :], 0.0))

            def inverse_table():
                setup(V.tensor_copy(INVW[:, 0, :], POW[:, 0:W]))
                setup(tt(INVW[:, 1, :], POW[:, 0:W], INVW[:, 0, :].bitcast(F32), SUB))

            def mixer_weights():
                setup(V.tensor_copy(MIXA[:, 0, :], MRE))
                setup(V.tensor_copy(MIXA[:, 1, :], MRE))
                setup(V.tensor_copy(MIXB[:, 1, :], MIM))
                setup(V.memset(MIXA[32:33, :, 0:1], 0.0))
                setup(V.memset(MIXB[32:33, 1:2, 0:1], 0.0))
                setup(ts(MIXB[:, 0, :], MIXB[:, 1, :], -1.0, None, MUL))

            def energy_weights():
                w2, w3 = P1[:, 3 * NV:4 * NV], P1[:, 4 * NV:5 * NV]
                setup(tt(w2, MIXA[:, 0, :], MIXA[:, 0, :], MUL))
                setup(tt(w3, MIXB[:, 1, :], MIXB[:, 1, :], MUL))
                setup(tt(w2, w2, w3, ADD))
                setup(ts(OMEGA[0:NU, 0, :], w2, 2.0, None, MUL))
                setup(tt(w3[:, 0:1], MIXA[:, 0, 0:1], MMIR[:, 0:1], MUL))
                setup(tt(w3[:, 1:2], MIXB[:, 1, 0:1], MMIR[:, 1:2], MUL))
                setup(tt(w3[:, 0:1], w3[:, 0:1], w3[:, 1:2], SUB))
                setup(tt(w3[:, 0:1], w3[:, 0:1], w2[:, 0:1], ADD))
                setup(ts(OMEGA[0:NU, 0, 0:1], w3[:, 0:1], 0.5, None, MUL))
                setup(V.tensor_copy(OMEGA[0:NU, 1, :], OMEGA[0:NU, 0, :]))

            def scalar_tables():
                setup(ts(OMEGA[64:128, 0, :], MIXA[:, 0, :], 2.0, None, MUL))
                setup(V.tensor_copy(OMEGA[64:128, 0, 0:1], MIXA[:, 0, 0:1]))
                setup(V.tensor_copy(OMEGA[64:128, 1, :], OMEGA[64:128, 0, :]))
                k, mw = SC[:, SC_K:SC_K + 1], SC[:, SC_MW:SC_MW + 1]
                setup(V.memset(WEIGHTS[0:64, :], 1.0))
                setup(ts(WEIGHTS[64:128, :], ONES[64:128, :], SC[64:128, SC_K:SC_K + 1], 2.0, MUL, MUL))
                setup(tt(KK[:, 1:2], k, k, MUL))
                setup(ts(KK[:, 2:3], k, -1.0, None, MUL))
                setup(tt(KK[:, 3:4], mw, mw, MUL))
                setup(ts(KK[:, 3:4], KK[:, 3:4], EPS, None, ADD))
                setup(tt(KK[:, 4:5], mw, SC[:, SC_OW:SC_OW + 1], MUL))
                tt(KK[:, 5:6], SC[:, SC_AB:SC_AB + 1], SC[:, SC_OB:SC_OB + 1], ADD).then_inc(setup_done, 1)
                dve.wait_ge(setup_done, 1)

            def sum_squares(nb, p):
                if not (isinstance(nb, int) and nb == 0 and p < 2):
                    dve.wait_ge(q_added, 32 * nb + p - 1)
                for n in (2 * p, 2 * p + 1):
                    dve.wait_ge(folded, 64 * nb + n + 1)
                    V.tensor_reduce(QP[:, n % 4, :], SQ[:, n % 4, 0:W].rearrange("p (g j) -> p g j", j=GW),
                                    AX.X, ADD).then_inc(q_summed, 1)

            def attend(b):
                dve.wait_ge(sums_made, b + 1)
                dve.wait_ge(q_added, 32 * b + 32)
                V.tensor_copy(STA[:, :], psB[0:IMGS, 0:64]).then_inc(sums_kept, 1)
                dve.wait_ge(totals_made, b + 1)
                n_g = 1.0 / (IMGS * H * GW)
                m, q, v, ve, rt, r = (MR[:, n, :] for n in (0, 1, 2, 3, 4, 5))
                step(ts(MR[:, 0:2, :].rearrange("p n g -> p (n g)"), psB[:, 64:128], n_g, None, MUL))
                step(tt(v, m, m, MUL))
                step(tt(v, q, v, SUB))
                ts(ve, v, 0.0, EPS, ALU.max, ADD).then_inc(gvar_made, 1)
                dve.wait_ge(groot_made, b + 1)
                step(V.reciprocal(r, rt))
                own = POW[:, 0:4 * 16]
                step(tt(own.rearrange("p (n c g) -> p n c g", n=2, c=WC),
                        over(MR[:, 0, 0:1], [[5 * GROUPS, 2], [16, WC], [1, 16]]),
                        over(GROUP[:, 0:1], [[0, 2], [0, WC], [1, 16]]), MUL))
                step(V.tensor_reduce(MW[:, 0:2, :].rearrange("p n c -> p (n c)"),
                                     own.rearrange("p (n g) -> p n g", g=16), AX.X, ADD))
                do(ts(MW[:, 2, :], MW[:, 0, :], float(H), None, MUL))
                for c in range(WC):
                    do(ts(GWR[:, c, :, :], GWT[:, c, :, :], MW[:, 1, c:c + 1], None, MUL))
                wait_link()
                for c in range(WC):
                    do(ts(Y[:, :, c, 0], Y[:, :, c, 0], MW[:, 2, c:c + 1], None, SUB))
                wait_link()
                V.memset(IM[:, 0:4], 0.0).then_inc(scaled_w, 1)
                step(tt(q, r, m, MUL))
                S, Q = STA[:, 0:32], STA[:, 32:64]
                t = [P1[0:IMGS, 32 * n:32 * (n + 1)] for n in range(4)]
                mr, rr = MR[0:IMGS, 0, 0:32], MR[0:IMGS, 5, 0:32]
                step(ts(t[0], mr, float(H * GW), None, MUL))
                step(tt(t[0], S, t[0], SUB))
                step(tt(t[1], t[0], rr, MUL))
                do(V.tensor_reduce(IM[:, 0:1], t[1], AX.X, ADD))
                step(tt(t[2], t[0], S, ADD))
                step(tt(t[2], t[2], mr, MUL))
                step(tt(t[2], Q, t[2], SUB))
                step(tt(t[2], t[2], rr, MUL))
                step(tt(t[2], t[2], rr, MUL))
                step(V.tensor_reduce(IM[:, 1:2], t[2], AX.X, ADD))
                step(ts(IM[:, 0:2], IM[:, 0:2], 1.0 / (H * W), None, MUL))
                step(tt(IM[:, 2:3], IM[:, 0:1], IM[:, 0:1], MUL))
                step(tt(IM[:, 2:3], IM[:, 1:2], IM[:, 2:3], SUB))
                ts(IM[:, 4:5], IM[:, 2:3], 0.0, EPS, ALU.max, ADD).then_inc(ivar_made, 1)
                for k in range(2):
                    p = 64 * k + NV
                    row = INVW[p:p + 1, :, :].rearrange("p k (g j) -> p k g j", j=GW)
                    src = over(MR[p:p + 1, 1, 0:32], [[1, 32], [0, GW]])
                    step(V.tensor_copy(row[:, 0], src))
                    do(tt(row[:, 1], src, row[:, 0].bitcast(F32), SUB))
                dve.wait_ge(iroot_made, 3 * b + 1)
                step(V.reciprocal(IM[:, 6:7], IM[:, 5:6]))
                step(tt(IM[:, 6:7], IM[:, 6:7], SC[0:IMGS, SC_N1W:SC_N1W + 1], MUL))
                dve.wait_ge(z_made, b + 1)
                Z = P1[0:IMGS, 128:128 + 16 * LU]
                for k in range(3):
                    n = min(8, LU - 8 * k)
                    do(V.tensor_copy(Z[:, 128 * k:128 * k + 16 * n].rearrange("p (n r v) -> p n r v", r=2, v=LV),
                                     psZ[k][0:IMGS, 0:64 * n].rearrange("p (n r v) -> p n r v", r=2, v=NV)
                                     [:, :, :, 0:LV]))
                wait_link()
                Zv = Z.rearrange("p (n r v) -> p n r v", r=2, v=LV)
                Xv = XL[:, :, :].rearrange("p r (u v) -> p r u v", v=LV)
                do(V.tensor_copy(Xv[:, :, 0, :], Zv[:, 0, :, :]))
                co = lambda r: Zv[:, 1:9, r, :]
                si = lambda r: Zv[:, 9:17, r, :]
                do(tt(Xv[:, 0, 1:9, :], co(0), si(1), ADD))
                do(tt(Xv[:, 1, 1:9, :], co(1), si(0), SUB))
                do(tt(Xv[:, 0, 16:8:-1, :], co(0), si(1), SUB))
                do(tt(Xv[:, 1, 16:8:-1, :], co(1), si(0), ADD))
                wait_link()
                step(ts(AT[:, :, :], XL[:, :, :], IM[:, 6:7], None, MUL))
                do(V.tensor_copy(AT[:, 0, 0:1], SC[0:IMGS, SC_N1B:SC_N1B + 1]))
                step(V.memset(AT[:, 1, 0:1], 0.0))

                def weights(n0, n1, t):
                    out = QKV[:, n0:n1, :, :]
                    for r, dst in enumerate((out, t)):
                        do(tt(dst, over(LW[:, n0, r, 0:1], [[2 * LOW, n1 - n0], [0, 2], [1, LOW]]),
                              over(AT[:, r, 0:1], [[0, n1 - n0], [LOW * (1 - 2 * r), 2], [1, LOW]]), MUL))
                    wait_link()
                    for r, op in enumerate((SUB, ADD)):
                        do(tt(out[:, :, r, :], out[:, :, r, :], t[:, :, r, :], op))
                    wait_link()

                def real_image(n):
                    val = QKV[:, n, :, :].rearrange("p r (u v) -> p r u v", v=LV)
                    e = P1[0:IMGS, 0:32].rearrange("p (r u) -> p r u", r=2)
                    for r in range(2):
                        do(tt(e[:, r, :], val[:, r, 1:17, 0], val[:, r, 16:0:-1, 0], SUB if r else ADD))
                    wait_link()
                    do(ts(val[:, :, 1:17, 0], e, 0.5, None, MUL))
                    do(V.memset(val[:, 1, 0, 0:1], 0.0))

                weights(0, 2, QKT)
                real_image(1)
                twice = QKV[:, 1, :, :].rearrange("p r (u v) -> p (r u) v", v=LV)[:, :, 1:LV]
                do(ts(twice, twice, 2.0, None, MUL))
                wait_link()
                V.memset(IM[:, 20:21], 0.0).then_inc(qk_ready, 1)
                weights(2, 3, VT)
                real_image(2)
                do(V.memset(QKV[:, 2, 0, 0:1], 0.0))
                do(ts(XL2, XL[:, :, :].rearrange("p r n -> p (r n)"), 2.0, None, MUL))
                wait_link()
                step(ts(XL2[:, ::LV], XL2[:, ::LV], 0.5, None, MUL))
                dve.wait_ge(logits_made, b + 1)
                step(V.tensor_reduce(IM[:, 7:8], psB[0:IMGS, 256:320], AX.X, ALU.max))
                ts(IM[:, 8:9], IM[:, 7:8], -LOGIT_SCALE, None, MUL).then_inc(max_made, 1)
                dve.wait_ge(exp_made, b + 1)
                step(V.reciprocal(IM[:, 10:11], IM[:, 9:10]))
                ts(PR[:, 0, :], PR[:, 0, :], IM[:, 10:11], None, MUL).then_inc(probs_made, 1)
                dve.wait_ge(att_squared, b + 1)
                cov = P1[0:IMGS, 0:2 * LOW]
                do(V.scalar_tensor_tensor(out=IM[:, 11:12], in0=IM[:, 18:19], scalar=2.0, in1=IM[:, 19:20],
                                          op0=MUL, op1=SUB))
                do(tt(cov, psT[1][0:IMGS, 0:2 * LOW], XL2, MUL))
                wait_link()
                ts(IM[:, 4:5], IM[:, 11:12], EPS, None, ADD).then_inc(ivar_made, 1)
                step(V.tensor_reduce(IM[:, 12:13], cov, AX.X, ADD))
                do(ts(IM[:, 15:16], IM[:, 12:13], 2.0, None, MUL))
                do(ts(P1[0:IMGS, 128:192], EYE[:, :], IM[:, 0:1], None, MUL))
                dve.wait_ge(iroot_made, 3 * b + 2)
                step(V.reciprocal(IM[:, 13:14], IM[:, 5:6]))
                step(tt(IM[:, 13:14], IM[:, 13:14], SC[0:IMGS, SC_AW:SC_AW + 1], MUL))
                step(V.scalar_tensor_tensor(out=IM[:, 14:15], in0=IM[:, 11:12], scalar=IM[:, 13:14],
                                            in1=IM[:, 15:16], op0=MUL, op1=ADD))
                step(V.scalar_tensor_tensor(out=IM[:, 14:15], in0=IM[:, 14:15], scalar=IM[:, 13:14],
                                            in1=IM[:, 2:3], op0=MUL, op1=ADD))
                ts(IM[:, 4:5], IM[:, 14:15], 0.0, EPS, ALU.max, ADD).then_inc(ivar_made, 1)
                step(ts(IM[:, 17:18], IM[:, 14:15], 0.0, None, ALU.max))
                do(ts(P1[0:IMGS, 192:256], EYE[:, :], IM[:, 13:14], None, MUL))
                do(ts(P1[0:IMGS, 64:128], EYE[:, :], IM[:, 17:18], None, MUL))
                dve.wait_ge(iroot_made, 3 * b + 3)
                step(V.reciprocal(IM[:, 16:17], IM[:, 5:6]))
                ts(P1[0:IMGS, 0:64], EYE[:, :], IM[:, 16:17], SC[0:IMGS, SC_N2W:SC_N2W + 1], MUL, MUL)\
                    .then_inc(diag_made, 1)
                dve.wait_ge(cb_kept, b + 1)
                dve.wait_ge(au_made, b + 1)
                for i0, i1 in ((0, G), (G, IMGS)):
                    for r in range(2):
                        tt(AU[:, i0:i1, r, :], psP[r][0:LU, :].rearrange("p (v i) -> p i v", v=LV)[:, i0:i1, :],
                           over(CB[64:64 + LU, 3, i0:i0 + 1], [[1, i1 - i0], [0, LV]]), MUL).then_inc(au_kept, 1)
                do(tt(A2Q[:, 0, :], CB[:, 0, :], CB[:, 0, :], MUL))
                do(ts(A2Q[:, 1, :], CB[:, 1, :], KK[:, 1:2], None, MUL))
                wait_link()

            def keep_low(b, n):
                for i in range(2):
                    src, dst = slice(64 * i, 64 * (i + 1)), slice(64 - 64 * i, 128 - 64 * i)
                    dve.wait_ge(t_high, 64 * b + 2 * n + 1 + i)
                    tt(T[dst, n % 2, i, :], psT[n % 2][src, 0:256], T[src, n % 2, i, :].bitcast(F32), SUB)\
                        .then_inc(t_kept, 1)

            def mix_products(b, g):
                dve.wait_ge(powers, 16 * b + 2 * g + 2)
                src = psX[0:NU, :].rearrange("p (i r v) -> p i r v", i=G, r=2)
                P1v = P1[:, :].rearrange("p (i r v) -> p i r v", i=G, r=2)
                dve.wait_ge(t_made, 32 * b + max(4 * g - 4, 0))
                P2v = S4[0:NU, g % 2, :, :].rearrange("p i (r v) -> p i r v", r=2)
                do(tt(P1v, src, over(MIXA[:, 0, 0:1], [[0, G], [NV, 2], [1, NV]]), MUL))
                wait_link()
                tt(P2v, src[:, :, ::-1, :], over(MIXB[:, 0, 0:1], [[0, G], [NV, 2], [1, NV]]), MUL)\
                    .then_inc(products, 1)

            def energies(b, g):
                dve.wait_ge(powers_weighted, 8 * b + g + 1)
                V.tensor_reduce(FP[:, :], POW[:, :].rearrange("p (i n) -> p i n", i=G), AX.X, ADD)\
                    .then_inc(energy_part, 1)

            def add_products(b, g):
                dve.wait_ge(products, 8 * b + g + 1)
                do(tt(P1[:, :], P1[:, :], S4[0:NU, g % 2, :, :].rearrange("p i n -> p (i n)"), ADD))

            def keep_energies(b, g):
                dve.wait_ge(energy_sum, 8 * b + g + 1)
                ps = psX if g else psT[0]
                do(V.tensor_copy(LO[:, :], ps[0:NU, 128:256]))
                ins = tt(CH[:, 3, :], ps[:, 0:G], A2Q[:, 1, G * g:G * (g + 1)], ADD)
                wait_link()
                ins.then_inc(energy_kept, 1)
                dve.wait_ge(energy_kept, 8 * b + g + 1)

            def variances(b, g):
                i0, i1 = G * g, G * (g + 1)
                c = [CH[:, n + (n > 0), :] for n in range(8)]
                step(V.scalar_tensor_tensor(out=c[3], in0=c[2], scalar=0.0, in1=A2Q[:, 0, i0:i1],
                                            op0=ALU.max, op1=MUL))
                ts(c[4], c[3], KK[:, 3:4], EPS * EPS, MUL, ADD).then_inc(var_made, 1)

            def coefficients(b, g):
                i0, i1 = G * g, G * (g + 1)
                c = [CH[:, n + (n > 0), :] for n in range(8)]
                dve.wait_ge(root_made, 8 * b + g + 1)
                step(V.reciprocal(c[6], c[5]))
                step(V.scalar_tensor_tensor(out=c[7], in0=c[6], scalar=KK[:, 4:5], in1=CB[:, 0, i0:i1],
                                            op0=MUL, op1=MUL))
                do(ts(c[2], c[7], SC[:, SC_K:SC_K + 1], 1.0, MUL, ADD))
                step(V.scalar_tensor_tensor(out=c[1], in0=c[7], scalar=KK[:, 2:3], in1=CB[:, 2, i0:i1],
                                            op0=MUL, op1=MUL))
                dve.wait_ge(x_scaled, 64 * b + max(8 * g - 8, 0))
                al = ALPHA[:, g % 2, :, :]
                do(tt(al, over(MR[:, 5, 0:1], [[0, G], [1, GROUPS]]), over(CH[:, 3, 0:1], [[1, G], [0, GROUPS]]), MUL))
                do(ts(CST[:, :, 0], c[1], KK[:, 5:6], None, ADD))
                do(ts(CST[:, :, 1], c[2], -1.0, None, MUL))
                wait_link()
                ts(al, al, 1.0, None, ADD).then_inc(alpha_made, 1)

            def mixed_modes(b, g):
                s = S4[0:NU, g % 2, :, :]
                lo = LO[:, :].rearrange("p (i n) -> p i n", i=G)
                do(tt(lo, lo, over(CH[0:NU, 3, 0:1], [[1, G], [0, 2 * LV]]), MUL))
                step(tt(s, P1[:, :].rearrange("p (i n) -> p i n", i=G), over(CH[0:NU, 8, 0:1], [[1, G], [0, 2 * NV]]), MUL))
                s_lo = s.rearrange("p i (r v) -> p i r v", r=2)[:, :, :, 0:LV]
                step(tt(s_lo, s_lo, lo.rearrange("p i (r v) -> p i r v", r=2), ADD))
                do(V.tensor_copy(S4[64:128, g % 2, :, 0:NV], s[:, :, NV:2 * NV]))
                step(ts(S4[64:128, g % 2, :, NV + 1:2 * NV], s[:, :, 1:NV], -1.0, None, MUL))
                step(V.memset(s[:, :, NV], 0.0))
                row = S4[32:33, g % 2, :, :].rearrange("p i (r v) -> p i r v", r=2)[:, :, :, 0]
                tt(row, row, CST[32:33, :, :], ADD).then_inc(s_made, 1)

            def finish(b, n):
                for a in range(HC):
                    if a == 0:
                        dve.wait_ge(x_scaled, 64 * b + 2 * n + 2)
                    dve.wait_ge(synth_made, 64 * b + 2 * n + a + 1)
                    v = X[:, 2 * n:2 * n + 2, a, :]
                    tt(v, v, psP[a][:, :].rearrange("p (i w) -> p i w", i=2), ADD).then_inc(out_made, 1)

            def produce(b, more):
                for g in range(NG + (LAG if more else 1)):
                    old, new, p0, q0 = 1 <= g <= NG, more and LAG <= g, PG * (g - 1), PG * (g - LAG)
                    if old:
                        keep_low(b, p0)
                        keep_low(b, p0 + 1)
                    if g < NG:
                        mix_products(b, g)
                        if old and not new:
                            finish(b, p0)
                        energies(b, g)
                    for j in range(PG):
                        if g < NG:
                            if j == 1:
                                add_products(b, g)
                                keep_energies(b, g)
                                variances(b, g)
                            if j == 3:
                                mixed_modes(b, g)
                        if old:
                            if new or j or g == NG:
                                finish(b, p0 + j)
                            if j < PG - 2:
                                keep_low(b, p0 + j + 2)
                        if g < NG and j == 2:
                            coefficients(b, g)
                        if new:
                            sum_squares(b + 1, q0 + j)

            setups = {4: inverse_table, 6: mixer_weights, 9: energy_weights, 12: scalar_tables}
            for p in range(PAIRS):
                if p == 4:
                    dve.wait_ge(tables_in, 16 * TABLES)
                if p in setups:
                    setups[p]()
                sum_squares(0, p)
            attend(0)
            produce(0, True)
            assert Chain.n == LINKS, Chain.n
            with dve.Fori(1, B - 1) as b:
                Chain.base, Chain.n = LINKS * b, 0
                attend(b)
                produce(b, True)
            Chain.base, Chain.n = LINKS * (B - 1), 0
            attend(B - 1)
            produce(B - 1, False)


def kernel(x, L0_conv_kw1, L0_conv_kw2, L0_conv_qw1, L0_conv_qw2, L0_conv_vw1, L0_conv_vw2, L0_conv_mix_w1,
           L0_conv_mix_w2, L0_conv_mix_bias, L0_conv_mix_skip_w, L0_conv_mix_skip_b, L0_conv_mix_norm_w,
           L0_conv_mix_norm_b, L0_conv_norm1_w, L0_conv_norm1_b, L0_conv_an_w, L0_conv_an_b, L0_conv_norm2_w,
           L0_conv_norm2_b, L0_conv_mon_w, L0_conv_mon_b):
    import concourse.bacc as bacc
    from concourse.bass_utils import run_bass_kernel_spmd

    def low(w1, w2):
        w1, w2 = np.asarray(w1)[0, 0], np.asarray(w2)[0, 0]
        rows = np.concatenate([w1, np.zeros((1,) + w1.shape[1:], w1.dtype), w2])
        return rows.transpose(2, 0, 1).reshape(-1)

    low_w = np.concatenate([low(L0_conv_qw1, L0_conv_qw2), low(L0_conv_kw1, L0_conv_kw2),
                            low(L0_conv_vw1, L0_conv_vw2)])
    w1, w2 = np.asarray(L0_conv_mix_w1)[0, 0], np.asarray(L0_conv_mix_w2)[0, 0]
    mix = np.concatenate([w2, w1])
    mirror = np.concatenate([np.zeros_like(mix[:1, 0]), mix[:0:-1, 0]])
    scal = np.concatenate([np.asarray(a).reshape(1) for a in (
        L0_conv_norm1_w, L0_conv_norm1_b, L0_conv_an_w, L0_conv_norm2_w, L0_conv_mix_skip_w,
        L0_conv_mix_norm_w, L0_conv_mon_w, L0_conv_an_b, L0_conv_mon_b)])
    arrays = {
        "in_x": np.ascontiguousarray(x),
        "in_mix_re": np.ascontiguousarray(mix[:, :, 0]), "in_mix_im": np.ascontiguousarray(mix[:, :, 1]),
        "in_mix_mirror": np.ascontiguousarray(mirror),
        "in_low_w": np.ascontiguousarray(np.broadcast_to(low_w, (IMGS, low_w.size))),
        "in_scalars": np.ascontiguousarray(np.broadcast_to(scal, (128, SCALARS))),
        **tables(),
    }
    nc = bacc.Bacc("TRN2", target_bir_lowering=False, num_devices=1)
    args = [nc.dram_tensor(n, a.shape, mybir.dt.from_np(a.dtype), kind="ExternalInput").ap()
            for n, a in arrays.items()]
    out = nc.dram_tensor("out", (B, IMGS, H, W), mybir.dt.float32, kind="ExternalOutput").ap()
    spectral_block(nc, *args, out)
    r = run_bass_kernel_spmd(nc, [arrays], core_ids=[0])
    return r.results[0]["out"]
```
